# Optimizing a Trainium2 kernel written in Bass

```python
import numpy as np
import jax
import jax.numpy as jnp

def _softmax(x, axis=-1):
    return jax.nn.softmax(x, axis=axis)

def _gelu(x):
    return jax.nn.gelu(x, approximate=True)

def _silu(x):
    return jax.nn.silu(x)

def _sigmoid(x):
    return jax.nn.sigmoid(x)

def _layernorm(x, axis=-1, eps=1e-05):
    m = jnp.mean(x, axis=axis, keepdims=True)
    v = jnp.var(x, axis=axis, keepdims=True)
    return (x - m) / jnp.sqrt(v + eps)

def _scatter_add(tgt, idx, src, axis=0):
    return tgt.at[idx].add(src)

def _segment_sum(src, seg, n):
    return jax.ops.segment_sum(src, seg, n)
kernel_name = 'mk_adaln_d1_jaxref_r8_c58ec4'

def setup_inputs(seed: int=0):
    np.random.seed(seed)
    _w = jnp.asarray

    def _L0_attn_setup():
        import jax, jax.numpy as jnp
        import numpy as np
        N_HEADS = 16
        HIDDEN = 128
        HEAD_DIM = 64
        BSZ = 4
        SEQ = 128
        SCALE = HEAD_DIM ** (-0.5)
        key = jax.random.key(seed)
        k_x, k_q, k_k, k_v, k_o = jax.random.split(key, 5)
        s = HIDDEN ** (-0.5)
        return {'x': jax.random.normal(k_x, (BSZ, SEQ, HIDDEN), dtype=jnp.float32), 'wq': jax.random.normal(k_q, (N_HEADS * HEAD_DIM, HIDDEN), dtype=jnp.float32) * s, 'wk': jax.random.normal(k_k, (N_HEADS * HEAD_DIM, HIDDEN), dtype=jnp.float32) * s, 'wv': jax.random.normal(k_v, (N_HEADS * HEAD_DIM, HIDDEN), dtype=jnp.float32) * s, 'wo': jax.random.normal(k_o, (HIDDEN, N_HEADS * HEAD_DIM), dtype=jnp.float32) * s}
    _L0_attn_in = _L0_attn_setup()

    def _L0_ffn_setup():
        import jax, jax.numpy as jnp
        import numpy as np
        B, T, C = (2, 128, 128)
        H = 512
        E_R, E_S, K = (8, 2, 2)

        def _rmsnorm(x, g):
            eps = jnp.finfo(x.dtype).eps
            return x * jax.lax.rsqrt(jnp.mean(x * x, axis=-1, keepdims=True) + eps) * g

        def _experts_mlp(x, g, W1, b1, W2, b2):
            xn = _rmsnorm(x, g)
            h = jnp.einsum('btc,ech->bteh', xn, W1) + b1
            h = jax.nn.gelu(h, approximate=False)
            return jnp.einsum('bteh,ehc->btec', h, W2) + b2
        key = jax.random.key(seed)
        ks = jax.random.split(key, 12)
        s = 0.02
        return {'u': jax.random.normal(ks[0], (B, T, C), dtype=jnp.float32), 'g_shared': jnp.ones((C,), jnp.float32), 'W1_s': jax.random.normal(ks[1], (E_S, C, H), jnp.float32) * s, 'b1_s': jax.random.normal(ks[2], (E_S, H), jnp.float32) * s, 'W2_s': jax.random.normal(ks[3], (E_S, H, C), jnp.float32) * s, 'b2_s': jax.random.normal(ks[4], (E_S, C), jnp.float32) * s, 'g_routed': jnp.ones((C,), jnp.float32), 'W1_r': jax.random.normal(ks[5], (E_R, C, H), jnp.float32) * s, 'b1_r': jax.random.normal(ks[6], (E_R, H), jnp.float32) * s, 'W2_r': jax.random.normal(ks[7], (E_R, H, C), jnp.float32) * s, 'b2_r': jax.random.normal(ks[8], (E_R, C), jnp.float32) * s, 'centroids': jax.random.normal(ks[9], (C, E_R), jnp.float32) * s}
    _L0_ffn_in = _L0_ffn_setup()
    _L0_c = _w((lambda *s: np.random.randn(*s).astype(np.float32) * 0.05)(8, 128))
    _L0_wmod = _w((lambda *s: np.random.randn(*s).astype(np.float32) * 0.05)(128, 6 * 128) * 128 ** (-0.5))
    _d = {'L0_attn_x': _L0_attn_in['x'], 'L0_attn_wq': _L0_attn_in['wq'], 'L0_attn_wk': _L0_attn_in['wk'], 'L0_attn_wv': _L0_attn_in['wv'], 'L0_attn_wo': _L0_attn_in['wo'], 'L0_ffn_g_shared': _L0_ffn_in['g_shared'], 'L0_ffn_W1_s': _L0_ffn_in['W1_s'], 'L0_ffn_b1_s': _L0_ffn_in['b1_s'], 'L0_ffn_W2_s': _L0_ffn_in['W2_s'], 'L0_ffn_b2_s': _L0_ffn_in['b2_s'], 'L0_ffn_g_routed': _L0_ffn_in['g_routed'], 'L0_ffn_W1_r': _L0_ffn_in['W1_r'], 'L0_ffn_b1_r': _L0_ffn_in['b1_r'], 'L0_ffn_W2_r': _L0_ffn_in['W2_r'], 'L0_ffn_b2_r': _L0_ffn_in['b2_r'], 'L0_ffn_centroids': _L0_ffn_in['centroids'], 'L0_c': _L0_c, 'L0_wmod': _L0_wmod}
    _x0 = _d['L0_attn_x']
    _d['L0_attn_x'] = jax.random.normal(jax.random.fold_in(jax.random.key(seed), 1), (8, 512, 128), dtype=_x0.dtype)
    del _x0
    return _d

def reference(L0_attn_x, L0_attn_wq, L0_attn_wk, L0_attn_wv, L0_attn_wo, L0_ffn_g_shared, L0_ffn_W1_s, L0_ffn_b1_s, L0_ffn_W2_s, L0_ffn_b2_s, L0_ffn_g_routed, L0_ffn_W1_r, L0_ffn_b1_r, L0_ffn_W2_r, L0_ffn_b2_r, L0_ffn_centroids, L0_c, L0_wmod):

    def _L0_attn_ref(x, wq, wk, wv, wo):
        import jax, jax.numpy as jnp
        import numpy as np
        N_HEADS = 16
        HIDDEN = 128
        HEAD_DIM = 64
        BSZ = 4
        SEQ = 128
        SCALE = HEAD_DIM ** (-0.5)
        bsz, seqlen, _ = x.shape
        xq = jnp.einsum('bsh,oh->bso', x, wq)
        xk = jnp.einsum('bsh,oh->bso', x, wk)
        xv = jnp.einsum('bsh,oh->bso', x, wv)
        xq = xq.reshape(bsz, N_HEADS, seqlen, HEAD_DIM)
        xk = xk.reshape(bsz, N_HEADS, seqlen, HEAD_DIM)
        xv = xv.reshape(bsz, N_HEADS, seqlen, HEAD_DIM)
        scores = jnp.einsum('bhid,bhjd->bhij', xq, xk) * SCALE
        scores = jax.nn.softmax(scores, axis=-1)
        out = jnp.einsum('bhij,bhjd->bhid', scores, xv)
        out = out.reshape(bsz, seqlen, N_HEADS * HEAD_DIM)
        return jnp.einsum('bso,ho->bsh', out, wo)

    def _L0_ffn_ref(u, g_shared, W1_s, b1_s, W2_s, b2_s, g_routed, W1_r, b1_r, W2_r, b2_r, centroids):
        import jax, jax.numpy as jnp
        import numpy as np
        B, T, C = (2, 128, 128)
        H = 512
        E_R, E_S, K = (8, 2, 2)

        def _rmsnorm(x, g):
            eps = jnp.finfo(x.dtype).eps
            return x * jax.lax.rsqrt(jnp.mean(x * x, axis=-1, keepdims=True) + eps) * g

        def _experts_mlp(x, g, W1, b1, W2, b2):
            xn = _rmsnorm(x, g)
            h = jnp.einsum('btc,ech->bteh', xn, W1) + b1
            h = jax.nn.gelu(h, approximate=False)
            return jnp.einsum('bteh,ehc->btec', h, W2) + b2
        h_s = _experts_mlp(u, g_shared, W1_s, b1_s, W2_s, b2_s).sum(axis=-2)
        scores = jax.nn.sigmoid(u @ centroids)
        gpk, i_topk = jax.lax.top_k(scores, K)
        gk = gpk / scores.sum(axis=-1, keepdims=True)
        routed_all = _experts_mlp(u, g_routed, W1_r, b1_r, W2_r, b2_r)
        routed_topk = jnp.take_along_axis(routed_all, i_topk[..., None], axis=2)
        h_r = (gk[..., None] * routed_topk).sum(axis=-2)
        return u + h_s + h_r
    x = L0_attn_x
    mod = (_silu(L0_c) @ L0_wmod).reshape(L0_c.shape[0], 6, 1, -1)
    sa, ca, ga, sb, cb, gb = (mod[:, 0], mod[:, 1], mod[:, 2], mod[:, 3], mod[:, 4], mod[:, 5])
    ga = (2 * (ga >= 0) - 1) * jnp.maximum(jnp.abs(ga), 0.25)
    gb = (2 * (gb >= 0) - 1) * jnp.maximum(jnp.abs(gb), 0.25)
    h = _layernorm(x, axis=-1) * (1 + ca) + sa
    x = x + ga * _L0_attn_ref(h, L0_attn_wq, L0_attn_wk, L0_attn_wv, L0_attn_wo)
    h = _layernorm(x, axis=-1) * (1 + cb) + sb
    x = x + gb * _L0_ffn_ref(h, L0_ffn_g_shared, L0_ffn_W1_s, L0_ffn_b1_s, L0_ffn_W2_s, L0_ffn_b2_s, L0_ffn_g_routed, L0_ffn_W1_r, L0_ffn_b1_r, L0_ffn_W2_r, L0_ffn_b2_r, L0_ffn_centroids)
    return x

_drawn_inputs = setup_inputs


def setup_inputs(seed=0):
    import zlib

    import numpy as np

    out = dict(_drawn_inputs(seed))
    spreads = {'L0_ffn_g_shared': (1.0, 0.6), 'L0_ffn_g_routed': (1.0, 0.6)}
    factors = {'L0_ffn_W1_s': 2.922,
     'L0_ffn_b1_s': 8.0,
     'L0_ffn_W2_s': 2.837,
     'L0_ffn_b2_s': 8.0,
     'L0_ffn_W1_r': 8.0,
     'L0_ffn_b1_r': 8.0,
     'L0_ffn_W2_r': 8.0,
     'L0_ffn_b2_r': 44.843,
     'L0_ffn_centroids': 8.0}
    for name, (base, spread) in spreads.items():
        noise = np.random.default_rng([zlib.crc32(name.encode()), seed]).standard_normal(out[name].shape)
        drawn = base * np.exp(spread * noise) if base else spread * noise
        out[name] = jnp.asarray(drawn.astype(out[name].dtype))
    for name, factor in factors.items():
        out[name] = (out[name] * factor).astype(out[name].dtype)
    return out
```

```python
from contextlib import ExitStack

import concourse.bass as bass
from concourse import mybir

F32 = mybir.dt.float32
F32R = mybir.dt.float32r
ACT = mybir.ActivationFunctionType
ALU = mybir.AluOpType
AX = mybir.AxisListType
ds = bass.ds

P = 128
BATCH, SEQ, C = 8, 512, 128
HEADS, DH = 16, 64
CHUNKS = HEADS
GT = SEQ // HEADS
NPOS = GT * CHUNKS
QUADS = BATCH * SEQ // P
GQ = P // GT
QB = SEQ // P
IT = NPOS // P
KQ = GQ * IT
PAIR = 2
KN = PAIR * KQ
GN = PAIR * GQ
E_S, E_R, HID = 2, 8, 512
E = E_S + E_R
HT = HID // P
EPS_LN = 1e-5
EPS_RMS = float(2.0 ** -23)
NEG = -1.0
TOPK = 2
RING_S, RING_T, RING_P = 2, 2, 4
STEPS = QUADS // PAIR
Y_AT = 7
RING_G, RING_O = 4, 3


class Count:

    def __init__(self, eng, n):
        self.eng, self.n = eng, n

    def __call__(self, sem, per, count):
        if isinstance(self.n, int):
            if self.n * per + count > 0:
                self.eng.wait_ge(sem, self.n * per + count)
        else:
            self.eng.wait_ge(sem, self.n * per + count)


def chain(eng, sem):
    seen = [0]

    def link(ins):
        seen[0] += 1
        ins.then_inc(sem, 1)
        eng.wait_ge(sem, seen[0])

    return link


def prepare(nc, t, dram):
    with ExitStack() as ctx:
        sem = lambda name: ctx.enter_context(nc.semaphore(name))
        sb = lambda name, shape, dt=F32: ctx.enter_context(nc.sbuf_tensor(name, shape, dt))
        loaded_x, loaded_c, loaded_w = sem("loaded_x"), sem("loaded_c"), sem("loaded_w")
        ident_ready, exp_c, silu_ready, modT_done, modB_done = map(
            sem, ("ident_ready", "exp_c", "silu_ready", "modT_done", "modB_done"))
        modB_copied, var_ready, std_ready, z_ready, zT_done, hT_ready = map(
            sem, ("modB_copied", "var_ready", "std_ready", "z_ready", "zT_done", "hT_ready"))
        dchain, achain, pchain = sem("dve_chain_a"), sem("act_chain_a"), sem("pool_chain_a")
        cT, sc, ec = sb("cT", [P, BATCH]), sb("sc", [P, BATCH]), sb("ec", [P, BATCH])
        scB = sb("scB", [P, BATCH, P])
        wmod = sb("wmod", [P, 6 * C])
        z = sb("z", [P, 2, QB, C])
        gsign = sb("gsign", [P, BATCH, C])
        pmod = ctx.enter_context(nc.psum_tensor("pmod", [P, 2, 512], F32))
        pT = ctx.enter_context(nc.psum_tensor("pT", [P, 2, 512], F32))
        pm = ctx.enter_context(nc.psum_tensor("pm", [P, 2, BATCH], F32))
        block = ctx.enter_context(nc.Block())

        @block.sync
        def _(sp):
            sp.dma_start(cT[:], dram["cT"]).then_inc(loaded_c, 16)
            sp.dma_start(wmod[:], dram["wmod"]).then_inc(loaded_c, 16)
            sp.dma_start(t["x"][:], dram["x"].rearrange("(q p) c -> p q c", p=P)).then_inc(loaded_x, 16)
            for half in range(2):
                rows = slice(half * DH, (half + 1) * DH)
                sp.dma_start(t["wq"][:, :, half, :], dram["wqT"].rearrange("p (k d) -> p k d", d=DH)).then_inc(loaded_w, 16)
                sp.dma_start(t["wk"][:, :, half, :], dram["wkT"].rearrange("p (k d) -> p k d", d=DH)).then_inc(loaded_w, 16)
                sp.dma_start(t["wo"][rows], dram["woT"].rearrange("d (k h) -> d k h", h=C)).then_inc(loaded_w, 16)
            sp.dma_start(t["wv"][:], dram["wvT"]).then_inc(loaded_w, 16)
            sp.wait_ge(loaded_w, 7 * 16)
            sp.wait_ge(loaded_x, 16)

        @block.gpsimd
        def _(pool):
            link = chain(pool, pchain)
            link(pool.memset(t["ident"][:], 0.0))
            pool.affine_select(out=t["ident"][:], in_=t["ident"][:], compare_op=ALU.not_equal, fill=1.0,
                               base=0, pattern=[[-1, P]], channel_multiplier=1).then_inc(ident_ready, 1)
            link(pool.memset(t["hT"][:, QUADS:QUADS + 2, :], 0.0))

        @block.scalar
        def _(act):
            act.wait_ge(loaded_c, 32)
            act.activation(ec[:], cT[:], ACT.Exp, scale=NEG).then_inc(exp_c, 1)
            for b in range(BATCH):
                act.wait_ge(modB_done, b + 1)
                act.activation(t["modB"][:, :, b, :], pmod[:, b % 2, :].rearrange("p (k c) -> p k c", c=C),
                               ACT.Copy).then_inc(modB_copied, 1)
            act.wait_ge(var_ready, 1)
            act.activation(t["rstd"][:], t["var"][:], ACT.Sqrt).then_inc(std_ready, 1)

        @block.tensor
        def _(pe):
            pe.wait_ge(silu_ready, 1)
            for k in range(2):
                mm = pe.matmul(pm[:, k, :], wmod[:, k * C:(k + 1) * C], sc[:], start=True, stop=True)
            mm.then_inc(modT_done, 1)
            pe.wait_ge(silu_ready, 2)
            for b in range(BATCH):
                if b >= 2:
                    pe.wait_ge(modB_copied, b - 1)
                pe.matmul(pmod[:, b % 2, :], scB[:, b, :], wmod[:, 2 * C:6 * C], start=True,
                          stop=True).then_inc(modB_done, 1)
            pe.wait_ge(ident_ready, 1)
            for b in range(BATCH):
                pe.wait_ge(z_ready, b + 1)
                if b >= 2:
                    pe.wait_ge(hT_ready, b - 1)
                for q in range(QB):
                    mm = pe.transpose(pT[:, b % 2, q * P:(q + 1) * P], z[:, b % 2, q, :], t["ident"][:])
                mm.then_inc(zT_done, 1)

        @block.vector
        def _(dve):
            link = chain(dve, dchain)
            dve.wait_ge(exp_c, 1)
            link(dve.tensor_scalar(ec[:], ec[:], 1.0, None, ALU.add))
            link(dve.reciprocal(ec[:], ec[:]))
            dve.tensor_tensor(sc[:], ec[:], cT[:], ALU.mult).then_inc(silu_ready, 1)
            dve.wait_ge(silu_ready, 1)
            dve.tensor_copy(scB[:], sc[:].unsqueeze(2).to_broadcast([P, BATCH, P])).then_inc(silu_ready, 1)
            dve.wait_ge(loaded_x, 16)
            layernorm_stats(dve, link, t)
            dve.tensor_scalar(t["var"][:], t["var"][:], EPS_LN, None, ALU.add).then_inc(var_ready, 1)
            dve.wait_ge(modT_done, 1)
            link(dve.tensor_copy(t["saT"][:], pm[:, 0, :]))
            link(dve.tensor_scalar(t["caT"][:], pm[:, 1, :], 1.0, None, ALU.add))
            dve.wait_ge(std_ready, 1)
            link(dve.reciprocal(t["rstd"][:], t["rstd"][:]))
            for b in range(BATCH + 1):
                if b < BATCH:
                    if b >= 2:
                        dve.wait_ge(zT_done, b - 1)
                    for q in range(QB):
                        k = b * QB + q
                        ins = dve.tensor_scalar(z[:, b % 2, q, :], t["x"][:, k, :], t["mean"][:, k:k + 1],
                                                t["rstd"][:, k:k + 1], ALU.subtract, ALU.mult)
                    ins.then_inc(z_ready, 1)
                if b >= 1:
                    dve.wait_ge(zT_done, b)
                    dve.tensor_scalar(t["hT"][:, (b - 1) * QB:b * QB, :].rearrange("p q c -> p (q c)"),
                                      pT[:, (b - 1) % 2, :], t["caT"][:, b - 1:b], t["saT"][:, b - 1:b],
                                      ALU.mult, ALU.add).then_inc(hT_ready, 1)
            dve.wait_ge(loaded_w, 7 * 16)
            link(dve.tensor_scalar(t["wq"][:], t["wq"][:], float(DH) ** -0.5, None, ALU.mult))
            dve.wait_ge(modB_copied, BATCH)
            for k in (0, 3):
                g = t["modB"][:, k, :, :]
                link(dve.tensor_scalar(gsign[:], g, 0.0, 2.0, ALU.is_ge, ALU.mult))
                link(dve.tensor_scalar(gsign[:], gsign[:], -1.0, None, ALU.add))
                link(dve.tensor_tensor(g, g, gsign[:], ALU.mult))
                link(dve.tensor_scalar(g, g, 0.25, None, ALU.max))
                link(dve.tensor_tensor(g, g, gsign[:], ALU.mult))
            link(dve.tensor_scalar(t["modB"][:, 2, :, :], t["modB"][:, 2, :, :], 1.0, None, ALU.add))


def layernorm_stats(dve, link, t):
    st = t["stats"]
    for q in range(QUADS):
        ins = dve.bn_stats(st[:, q, :], t["x"][:, q, :])
    link(ins)
    me, m2e, mo, m2o = (st[:, :, k] for k in (1, 2, 4, 5))
    link(dve.tensor_tensor(t["mean"][:], me, mo, ALU.add))
    link(dve.tensor_tensor(t["var"][:], me, mo, ALU.subtract))
    link(dve.tensor_scalar(t["mean"][:], t["mean"][:], 0.5, None, ALU.mult))
    link(dve.scalar_tensor_tensor(out=t["var"][:], in0=t["var"][:], scalar=C / 4.0, in1=t["var"][:],
                                  op0=ALU.mult, op1=ALU.mult))
    link(dve.tensor_tensor(t["var"][:], t["var"][:], m2e, ALU.add))
    link(dve.tensor_tensor(t["var"][:], t["var"][:], m2o, ALU.add))
    link(dve.tensor_scalar(t["var"][:], t["var"][:], 1.0 / C, None, ALU.mult))


def attend(nc, t):
    with ExitStack() as ctx:
        sem = lambda name: ctx.enter_context(nc.semaphore(name))
        sb = lambda name, shape, dt=F32: ctx.enter_context(nc.sbuf_tensor(name, shape, dt))
        psum = lambda name, n: ctx.enter_context(nc.psum_tensor(name, [P, n, 512], F32))
        hq_ready, y_done, y_out = sem("hq_ready"), sem("y_done"), sem("y_out")
        q_done, k_done, v_done = sem("q_done"), sem("k_done"), sem("v_done")
        q_hi, k_hi, v_hi = sem("q_hi"), sem("k_hi"), sem("v_hi")
        q_lo, k_lo, v_lo = sem("q_lo"), sem("k_lo"), sem("v_lo")
        pv_done, o_out = sem("pv_done"), sem("o_out")
        s_done, max_done, exp_done, rden_done, p_scaled, t_done, t_hi, t_lo = map(
            sem, ("s_done", "max_done", "exp_done", "rden_done", "p_scaled", "t_done", "t_hi", "t_lo"))

        pool_turn = sem("pool_turn")

        hq = sb("hq", [P, 2, P])
        Q = sb("Q", [P, 2, GQ, NPOS], F32R)
        KH = sb("KH", [P, 2, GQ, NPOS], F32R)
        KL = sb("KL", [P, 2, GQ, NPOS], F32R)
        V = sb("V", [P, 2, GQ, IT, 2, DH], F32R)
        prob = sb("prob", [P, RING_P, NPOS])
        PH = sb("PH", [P, 2, IT, NPOS], F32R)
        PL = sb("PL", [P, 2, IT, NPOS], F32R)
        O = sb("O", [P, CHUNKS, P])
        nmax, den, rden = (sb(name, [P, RING_P]) for name in ("nmax", "den", "rden"))
        ps_s, ps_t, ps_o, ps_qv, ps_k, ps_y = (
            psum("ps_s", RING_S), psum("ps_t", RING_T), psum("ps_o", 1), psum("ps_qv", 1), psum("ps_k", 1),
            psum("ps_y", 1))
        hT, ident = t["hT"], t["ident"]

        def within(n, per, index):
            return not isinstance(n, int) or 0 <= n * per + index < STEPS * per

        def project(pe, n, k):
            cnt, g, i = Count(pe, n), k // IT, k % IT
            nxt, slot = 1 - (g // GQ) % 2, g % GQ
            if i < 2:
                w, bank = ((t["wq"], ps_qv), (t["wk"], ps_k))[i]
                if i == 0:
                    cnt(v_lo, GN, g + GQ)
                    if slot == 0:
                        cnt(hq_ready, PAIR, g // GQ + 2)
                else:
                    cnt(k_lo, GN, g + GQ)
                for c in range(4):
                    mm = pe.matmul(bank[:, 0, c * P:(c + 1) * P],
                                   w[:, 4 * slot + c, :, :].rearrange("p a d -> p (a d)"), hq[:, nxt, :],
                                   start=True, stop=True)
                mm.then_inc((q_done, k_done)[i], 1)
            elif i == 2:
                cnt(q_lo, GN, g + GQ + 1)
                wv = t["wv"][:].rearrange("p (a c d) -> p c a d", c=4, d=DH)
                for c in range(4):
                    mm = pe.matmul(ps_qv[c * GT:(c + 1) * GT, 0, 0:IT * DH],
                                   hq[:, nxt, slot * GT:(slot + 1) * GT], wv[:, c], start=True, stop=True,
                                   tile_position=(0, c * GT))
                mm.then_inc(v_done, 1)

        def pe_tile(pe, n, k):
            cnt, g, i = Count(pe, n), k // IT, k % IT
            if within(n, KN, k):
                par, slot = (g // GQ) % 2, g % GQ
                if k % KQ == 0:
                    cnt(q_lo, GN, g + GQ)
                    cnt(k_lo, GN, g + GQ)
                cnt(exp_done, KN, k - RING_S + 1)
                for part in (KH, KL):
                    mm = pe.matmul(ps_s[:, k % RING_S, :], Q[:, par, slot, i * P:(i + 1) * P],
                                   part[:, par, slot, :], start=(part is KH), stop=(part is KL))
                mm.then_inc(s_done, 1)
                project(pe, n, k)
            kt = k - 2
            if within(n, KN, kt):
                cnt(p_scaled, KN, kt + 1)
                cnt(t_lo, KN, kt - RING_T + 1)
                for a in range(IT):
                    mm = pe.transpose(ps_t[:, kt % RING_T, a * P:(a + 1) * P],
                                      prob[:, kt % RING_P, a * P:(a + 1) * P], ident[:])
                mm.then_inc(t_done, 1)
            if i in (3, 0):
                gt, a0 = (g - 1, 0) if i == 3 else (g - 2, 2)
                if within(n, GN, gt):
                    if a0 == 0:
                        cnt(t_lo, KN, IT * (gt + 1))
                        cnt(v_lo, GN, gt + 1)
                        cnt(o_out, GN, gt)
                    par, slot = (gt // GQ) % 2, gt % GQ
                    for a in (a0, a0 + 1):
                        for part in (PH, PL):
                            mm = pe.matmul(ps_o[:, 0, :], V[:, par, slot, a].rearrange("p h d -> p (h d)"),
                                           part[:, gt % 2, a, :], start=(a == 0 and part is PH),
                                           stop=(a == IT - 1 and part is PL))
                    if a0:
                        mm.then_inc(pv_done, 1)
            qt = k // KQ - 1
            if k % KQ == Y_AT and within(n, PAIR, qt):
                cnt(o_out, GN, GQ * (qt + 1))
                cnt(y_out, PAIR, qt)
                for c in range(CHUNKS):
                    mm = pe.matmul(ps_y[:, 0, 0:C], O[:, c, :], t["wo"][:, c, :], start=(c == 0),
                                   stop=(c == CHUNKS - 1))
                mm.then_inc(y_done, 1)

        def by_group(ap):
            return ap.rearrange("p (c g t) -> p c g t", c=4, g=GQ)

        def into_groups(buf, par, slot, rows=slice(0, P)):
            return buf[rows, par, :, 4 * slot * GT:4 * (slot + 1) * GT].rearrange("p g (c t) -> p c g t", c=4)

        def act_project(act, n, k):
            cnt, g, i = Count(act, n), k // IT, k % IT
            nxt, slot = 1 - (g // GQ) % 2, g % GQ
            if i < 2:
                done, ready, buf, bank = ((q_done, q_hi, Q, ps_qv), (k_done, k_hi, KH, ps_k))[i]
                cnt(done, GN, g + GQ + 1)
                act.activation(into_groups(buf, nxt, slot), by_group(bank[:, 0, :]), ACT.Copy).then_inc(ready, 1)
            elif i == 2:
                cnt(v_done, GN, g + GQ + 1)
                cnt(pv_done, GN, g - GQ + 1)
                act.activation(V[:, nxt, slot, :, 0, :], ps_qv[:, 0, 0:IT * DH].rearrange("p (a d) -> p a d", d=DH),
                               ACT.Copy).then_inc(v_hi, 1)

        def act_tile(act, n, k):
            cnt, g, i = Count(act, n), k // IT, k % IT
            if within(n, KN, k):
                cnt(max_done, KN, k + 1)
                cnt(t_done, KN, k - RING_P + 1)
                r = k % RING_P
                act.activation(prob[:, r, :], ps_s[:, k % RING_S, :], ACT.Exp, bias=nmax[:, r:r + 1],
                               accum_out=den[:, r:r + 1]).then_inc(exp_done, 1)
                act_project(act, n, k)
            kt = k - 2
            if within(n, KN, kt):
                gt, it = kt // IT, kt % IT
                cnt(t_done, KN, kt + 1)
                if it == 0:
                    cnt(pv_done, GN, gt - 1)
                act.activation(PH[:, gt % 2, :, it * P:(it + 1) * P],
                               ps_t[:, kt % RING_T, :].rearrange("p (a q) -> p a q", a=IT),
                               ACT.Copy).then_inc(t_hi, 1)
            gt = g - 2
            if i == 1 and within(n, GN, gt):
                slot = gt % GQ
                cnt(pv_done, GN, gt + 1)
                if slot == 0:
                    cnt(y_done, PAIR, gt // GQ)
                act.activation(O[:, :, slot * GT:(slot + 1) * GT],
                               ps_o[:, 0, :].rearrange("p (c t) -> p c t", t=GT), ACT.Copy).then_inc(o_out, 1)

        def dve_project(dve, n, k):
            cnt, g, i = Count(dve, n), k // IT, k % IT
            nxt, slot = 1 - (g // GQ) % 2, g % GQ
            if i == 0:
                low = slice(DH, P)
                cnt(q_hi, GN, g + GQ + 1)
                dst = into_groups(Q, nxt, slot, low)
                dve.tensor_tensor(dst, by_group(ps_qv[low, 0, :]), dst, ALU.subtract).then_inc(q_lo, 1)
            elif i == 1:
                cnt(k_hi, GN, g + GQ + 1)
                dve.tensor_tensor(into_groups(KL, nxt, slot), by_group(ps_k[:, 0, :]),
                                  into_groups(KH, nxt, slot), ALU.subtract).then_inc(k_lo, 1)
            elif i == 2:
                cnt(v_hi, GN, g + GQ + 1)
                dve.tensor_tensor(V[:, nxt, slot, :, 1, :], ps_qv[:, 0, 0:IT * DH].rearrange("p (a d) -> p a d", d=DH),
                                  V[:, nxt, slot, :, 0, :], ALU.subtract).then_inc(v_lo, 1)

        def dve_tile(dve, n, k):
            cnt = Count(dve, n)
            if within(n, KN, k):
                cnt(s_done, KN, k + 1)
                dve.tensor_reduce(nmax[:, k % RING_P:k % RING_P + 1], ps_s[:, k % RING_S, :], AX.X, ALU.max,
                                  negate=True).then_inc(max_done, 1)
            kt = k - 3
            if within(n, KN, kt):
                gt, it = kt // IT, kt % IT
                cnt(t_hi, KN, kt + 1)
                dve.tensor_tensor(PL[:, gt % 2, :, it * P:(it + 1) * P],
                                  ps_t[:, kt % RING_T, :].rearrange("p (a q) -> p a q", a=IT),
                                  PH[:, gt % 2, :, it * P:(it + 1) * P], ALU.subtract).then_inc(t_lo, 1)
            if within(n, KN, k):
                r = k % RING_P
                cnt(exp_done, KN, k + 1)
                dve.reciprocal(rden[:, r:r + 1], den[:, r:r + 1]).then_inc(rden_done, 1)
                dve_project(dve, n, k)
            qt = k // KQ - 1
            if k % KQ == Y_AT + 1 and within(n, PAIR, qt):
                cnt(y_done, PAIR, qt + 1)
                dve.tensor_copy(hT[:, ds(n * PAIR + qt, 1), :].rearrange("p q c -> p (q c)"),
                                ps_y[:, 0, 0:C]).then_inc(y_out, 1)

        def pool_tile(pool, n, k):
            cnt, r = Count(pool, n), k % RING_P
            cnt(rden_done, KN, k + 1)
            pool.sem_inc(pool_turn, 1)
            pool.tensor_scalar(prob[:, r, :], prob[:, r, :], rden[:, r:r + 1], 1.0, ALU.mult,
                               ALU.mult).then_inc(p_scaled, 1)
            if k % KQ == 1:
                quad = k // KQ
                cnt(v_done, GN, GQ * (quad + 1))
                pool.tensor_copy(hq[:, quad, :], hT[:, ds(n * PAIR + quad + 2, 1), :].rearrange("p q c -> p (q c)")
                                 ).then_inc(hq_ready, 1)

        def steps(eng, tile):
            for k in range(KN):
                tile(eng, 0, k)
            with eng.Fori(1, STEPS) as n:
                for k in range(KN):
                    tile(eng, n, k)

        block = ctx.enter_context(nc.Block())

        @block.tensor
        def _(pe):
            for k in range(KQ, KN):
                project(pe, -1, k)
            steps(pe, pe_tile)
            for k in range(Y_AT + 2):
                pe_tile(pe, STEPS, k)

        @block.scalar
        def _(act):
            for k in range(KQ, KN):
                act_project(act, -1, k)
            steps(act, act_tile)
            for k in range(Y_AT + 2):
                act_tile(act, STEPS, k)

        @block.vector
        def _(dve):
            for k in range(KQ, KN):
                dve_project(dve, -1, k)
            steps(dve, dve_tile)
            for k in range(Y_AT + 2):
                dve_tile(dve, STEPS, k)

        @block.gpsimd
        def _(pool):
            for quad in range(2):
                pool.tensor_copy(hq[:, quad, :], hT[:, quad, :]).then_inc(hq_ready, 1)
            steps(pool, pool_tile)


def route(nc, t, dram):
    with ExitStack() as ctx:
        sem = lambda name: ctx.enter_context(nc.semaphore(name))
        sb = lambda name, shape, dt=F32: ctx.enter_context(nc.sbuf_tensor(name, shape, dt))
        (w1_loaded, w_loaded, lower_ready, var_ready, std_ready, u_ready, ms_ready, mse_ready, rms_ready, un_ready,
         tr_done, uT_ready, unT_ready, logit_done, logit_ready, expl) = map(
            sem, ("w1_loaded", "w_loaded", "lower_ready", "var_ready2", "std_ready2", "u_ready", "ms_ready", "mse_ready",
                  "rms_ready", "un_ready", "tr_done", "uT_ready", "unT_ready", "logit_done", "logit_ready", "expl"))
        dchain, pchain = sem("dve_chain_c"), sem("pool_chain_c")
        z = sb("z2", [P, 2, QB, C])
        sq = sb("sq", [P, 2, C])
        un = sb("un", [P, 2, QB, C])
        ms, rr = sb("ms", [P, QUADS]), sb("rr", [P, QUADS])
        uT = sb("uT", [P, 2, 512])
        logit = sb("logit", [P, QUADS, E_R])
        lower = sb("lower", [P, E_R, E_R])
        gt_, eq = sb("gt_", [P, QUADS, E_R, E_R]), sb("eq", [P, QUADS, E_R, E_R])
        rank, ssum = sb("rank", [P, QUADS, E_R]), sb("ssum", [P, QUADS])
        p_u = ctx.enter_context(nc.psum_tensor("p_u", [P, 2, 512], F32))
        p_n = ctx.enter_context(nc.psum_tensor("p_n", [P, 2, 512], F32))
        p_l = ctx.enter_context(nc.psum_tensor("p_l", [P, 2, 512], F32))
        block = ctx.enter_context(nc.Block())
        x, y = t["x"], t["hT"]

        @block.sync
        def _(sp):
            for name in ("cent", "g2"):
                sp.dma_start(t[name][:], dram[name]).then_inc(w_loaded, 16)
            for e in range(E_S):
                sp.dma_start(t["w1"][:, e, :], dram["w1s"][e]).then_inc(w1_loaded, 16)
                sp.dma_start(t["w2"][:, e, :, :], dram["w2s"][e].rearrange("(h p) c -> p h c", p=P)).then_inc(w_loaded, 16)
            for e in range(E_R):
                sp.dma_start(t["w1"][:, E_S + e, :], dram["w1r"][e]).then_inc(w1_loaded, 16)
                sp.dma_start(t["w2"][:, E_S + e, :, :], dram["w2r"][e].rearrange("(h p) c -> p h c", p=P)).then_inc(w_loaded, 16)
            sp.dma_start(t["b1"][:, 0:E_S * HT], dram["b1s"]).then_inc(w_loaded, 16)
            sp.dma_start(t["b1"][:, E_S * HT:], dram["b1r"]).then_inc(w_loaded, 16)
            sp.dma_start(t["b2"][0:E_S, :], dram["b2s"]).then_inc(w_loaded, 16)
            sp.dma_start(t["b2"][E_S:E, :], dram["b2r"]).then_inc(w_loaded, 16)
            sp.wait_ge(w_loaded, 16 * (6 + E))

        @block.gpsimd
        def _(pool):
            link = chain(pool, pchain)
            link(pool.memset(lower[:], 1.0))
            pool.affine_select(out=lower[:], in_=lower[:], compare_op=ALU.is_gt, fill=0.0, base=0,
                               pattern=[[1, E_R], [-1, E_R]], channel_multiplier=0).then_inc(lower_ready, 1)

        @block.scalar
        def _(act):
            act.wait_ge(var_ready, 1)
            act.activation(t["rstd"][:], t["var"][:], ACT.Sqrt).then_inc(std_ready, 1)
            for k in range(QUADS):
                if k % QB == 0:
                    act.wait_ge(u_ready, k // QB + 1)
                if k >= 2:
                    act.wait_ge(ms_ready, k - 1)
                act.activation(sq[:, k % 2, :], t["u"][:, k, :], ACT.Square, accum_out=ms[:, k:k + 1]).then_inc(ms_ready, 1)
            act.wait_ge(mse_ready, 1)
            act.activation(rr[:], rr[:], ACT.Sqrt).then_inc(rms_ready, 1)
            for b in range(BATCH + 1):
                if b < BATCH:
                    act.wait_ge(tr_done, b + 1)
                    if b >= 2:
                        act.wait_ge(logit_done, b - 1)
                    act.activation(uT[:, b % 2, :], p_u[:, b % 2, :], ACT.Copy).then_inc(uT_ready, 1)
                if b >= 1:
                    act.wait_ge(logit_done, b)
                    act.activation(logit[:, (b - 1) * QB:b * QB, :],
                                   p_l[:, (b - 1) % 2, 0:QB * E_R].rearrange("p (q e) -> p q e", e=E_R),
                                   ACT.Copy).then_inc(logit_ready, 1)
            act.wait_ge(logit_ready, BATCH)
            act.activation(logit[:], logit[:], ACT.Exp, scale=NEG).then_inc(expl, 1)

        @block.tensor
        def _(pe):
            pe.wait_ge(w_loaded, 16 * (6 + E))
            for b in range(BATCH + 1):
                if b < BATCH:
                    pe.wait_ge(un_ready, b + 1)
                    if b >= 2:
                        pe.wait_ge(uT_ready, b - 1)
                        pe.wait_ge(unT_ready, b - 1)
                    for q in range(QB):
                        pe.transpose(p_u[:, b % 2, q * P:(q + 1) * P], t["u"][:, b * QB + q, :], t["ident"][:])
                        mm = pe.transpose(p_n[:, b % 2, q * P:(q + 1) * P], un[:, b % 2, q, :], t["ident"][:])
                    mm.then_inc(tr_done, 1)
                if b >= 1:
                    pe.wait_ge(uT_ready, b)
                    if b >= 3:
                        pe.wait_ge(logit_ready, b - 2)
                    for q in range(QB):
                        mm = pe.matmul(p_l[:, (b - 1) % 2, q * E_R:(q + 1) * E_R], uT[:, (b - 1) % 2, q * P:(q + 1) * P],
                                       t["cent"][:], start=True, stop=True)
                    mm.then_inc(logit_done, 1)

        @block.vector
        def _(dve):
            link = chain(dve, dchain)

            def spread(k, b):
                return t["modB"][:, k, b, :].unsqueeze(1).to_broadcast([P, QB, C])

            for b in range(BATCH):
                yb = y[:, b * QB:(b + 1) * QB, :]
                ins = dve.tensor_tensor(yb, yb, spread(0, b), ALU.mult)
            link(ins)
            for b in range(BATCH):
                sl = slice(b * QB, (b + 1) * QB)
                ins = dve.tensor_tensor(x[:, sl, :], x[:, sl, :], y[:, sl, :], ALU.add)
            link(ins)
            layernorm_stats(dve, link, t)
            dve.tensor_scalar(t["var"][:], t["var"][:], EPS_LN, None, ALU.add).then_inc(var_ready, 1)
            dve.wait_ge(std_ready, 1)
            link(dve.reciprocal(t["rstd"][:], t["rstd"][:]))
            for b in range(BATCH):
                sl = slice(b * QB, (b + 1) * QB)
                for k in range(b * QB, (b + 1) * QB):
                    ins = dve.tensor_scalar(z[:, b % 2, k % QB, :], x[:, k, :], t["mean"][:, k:k + 1],
                                            t["rstd"][:, k:k + 1], ALU.subtract, ALU.mult)
                link(ins)
                link(dve.tensor_tensor(t["u"][:, sl, :], z[:, b % 2, :, :], spread(2, b), ALU.mult))
                dve.tensor_tensor(t["u"][:, sl, :], t["u"][:, sl, :], spread(1, b), ALU.add).then_inc(u_ready, 1)
            dve.wait_ge(ms_ready, QUADS)
            dve.tensor_scalar(rr[:], ms[:], 1.0 / C, EPS_RMS, ALU.mult, ALU.add).then_inc(mse_ready, 1)
            dve.wait_ge(rms_ready, 1)
            link(dve.reciprocal(rr[:], rr[:]))
            for b in range(BATCH + 1):
                if b < BATCH:
                    if b >= 2:
                        dve.wait_ge(tr_done, b - 1)
                    for k in range(b * QB, (b + 1) * QB):
                        ins = dve.tensor_scalar(un[:, b % 2, k % QB, :], t["u"][:, k, :], rr[:, k:k + 1], None, ALU.mult)
                    ins.then_inc(un_ready, 1)
                if b >= 1:
                    dve.wait_ge(tr_done, b)
                    dve.tensor_copy(t["unT"][:, (b - 1) * 512:b * 512], p_n[:, (b - 1) % 2, :]).then_inc(unT_ready, 1)
            dve.wait_ge(w1_loaded, 16 * E)
            dve.wait_ge(w_loaded, 16 * (6 + E))
            link(dve.tensor_scalar(t["w1"][:, 0:E_S, :], t["w1"][:, 0:E_S, :], t["g2"][:, 0:1], None, ALU.mult))
            link(dve.tensor_scalar(t["w1"][:, E_S:E, :], t["w1"][:, E_S:E, :], t["g2"][:, 1:2], None, ALU.mult))
            dve.wait_ge(expl, 1)
            score = logit
            link(dve.tensor_scalar(score[:], score[:], 1.0, None, ALU.add))
            link(dve.reciprocal(score[:], score[:]))
            link(dve.tensor_reduce(ssum[:], score[:], AX.X, ALU.add))
            link(dve.reciprocal(ssum[:], ssum[:]))
            this = score[:].unsqueeze(3).to_broadcast([P, QUADS, E_R, E_R])
            other = score[:].unsqueeze(2).to_broadcast([P, QUADS, E_R, E_R])
            link(dve.tensor_tensor(gt_[:], other, this, ALU.is_gt))
            link(dve.tensor_tensor(eq[:], other, this, ALU.is_equal))
            dve.wait_ge(lower_ready, 1)
            flat = "p e f -> p (e f)"
            link(dve.tensor_tensor(eq[:].rearrange("p q e f -> p q (e f)"), eq[:].rearrange("p q e f -> p q (e f)"),
                                   lower[:].rearrange(flat).unsqueeze(1).to_broadcast([P, QUADS, E_R * E_R]), ALU.mult))
            link(dve.tensor_tensor(gt_[:], gt_[:], eq[:], ALU.add))
            link(dve.tensor_reduce(rank[:], gt_[:], AX.X, ALU.add))
            link(dve.scalar_tensor_tensor(out=rank[:], in0=rank[:], scalar=TOPK - 0.5, in1=score[:], op0=ALU.is_lt,
                                          op1=ALU.mult))
            link(dve.memset(t["gate"][:, :, 0:E_S], 1.0))
            link(dve.tensor_tensor(t["gate"][:, :, E_S:E], rank[:], ssum[:].unsqueeze(2).to_broadcast([P, QUADS, E_R]),
                                   ALU.mult))


def mix(nc, t, dram):
    with ExitStack() as ctx:
        sem = lambda name: ctx.enter_context(nc.semaphore(name))
        sb = lambda name, shape, dt=F32: ctx.enter_context(nc.sbuf_tensor(name, shape, dt))
        h_done, g_ready, w2_done, out_taken, gq_ready, gT_done, gT_ready, acc_ready, res_ready, stored = map(
            sem, ("h_done", "g_ready", "w2_done", "out_taken", "gq_ready", "gT_done", "gT_ready", "acc_ready",
                  "res_ready", "stored"))
        G = sb("G", [P, RING_G, 512])
        acc = sb("acc", [P, QB, C])
        res = sb("res", [P, QB, C])
        gq = sb("gq", [P, QB, E])
        gT = sb("gT", [E, QB, P])
        p_h = ctx.enter_context(nc.psum_tensor("p_h", [P, RING_G, 512], F32))
        p_o = ctx.enter_context(nc.psum_tensor("p_o", [P, RING_O, 512], F32))
        p_g = ctx.enter_context(nc.psum_tensor("p_g", [P, 512], F32))
        block = ctx.enter_context(nc.Block())
        units = [(e, h) for e in range(E) for h in range(HT)]
        U = len(units)
        SUMS = 1 + E_R
        sum_of = lambda e: max(0, e - E_S + 1)
        closes = lambda u: units[u][1] == HT - 1 and units[u][0] >= E_S - 1

        @block.gpsimd
        def _(pool):
            with pool.Fori(0, BATCH) as b:
                pool.wait_ge(gT_done, b + 1)
                pool.tensor_copy(gq[:], t["gate"][:, ds(b * QB, QB), :]).then_inc(gq_ready, 1)

        @block.tensor
        def _(pe):
            pe.sem_inc(w2_done, RING_G)
            pe.sem_inc(gT_done, 1)
            with pe.Fori(0, BATCH) as b:
                pe.wait_ge(gq_ready, b + 1)
                for q in range(QB):
                    mm = pe.transpose(p_g[0:E, q * P:(q + 1) * P], gq[:, q, :], t["ident"][:])
                mm.then_inc(gT_done, 1)

                def second(u):
                    e, h = units[u]
                    s = sum_of(e)
                    first = h == 0 and e in (0, *range(E_S, E))
                    if first:
                        pe.wait_ge(out_taken, b * SUMS + s + 1)
                    if u == 0:
                        pe.wait_ge(gT_ready, b + 1)
                        for q in range(QB):
                            pe.matmul(p_o[:, s % RING_O, q * P:(q + 1) * P], gT[:, q, :], t["b2"][:], start=(q == 0),
                                      stop=False, skip_group_check=True)
                    pe.wait_ge(g_ready, b * U + u + 1)
                    for q in range(QB):
                        mm = pe.matmul(p_o[:, s % RING_O, q * P:(q + 1) * P], G[:, u % RING_G, q * P:(q + 1) * P],
                                       t["w2"][:, e, h, :], start=(first and q == 0 and u > 0), stop=closes(u),
                                       skip_group_check=True)
                    mm.then_inc(w2_done, 1)

                for u in range(U + 1):
                    if u < U:
                        e, h = units[u]
                        pe.matmul(p_h[:, u % RING_G, :], t["w1"][:, e, h * P:(h + 1) * P],
                                  t["unT"][:, ds(b * 512, 512)], start=True, stop=True).then_inc(h_done, 1)
                    if u >= 1:
                        second(u - 1)

        @block.scalar
        def _(act):
            with act.Fori(0, BATCH) as b:
                for u in range(U):
                    act.wait_ge(w2_done, b * U + u + 1)
                    act.wait_ge(h_done, b * U + u + 1)
                    act.activation(G[:, u % RING_G, :], p_h[:, u % RING_G, :], ACT.Gelu,
                                   bias=t["b1"][:, u:u + 1]).then_inc(g_ready, 1)

        @block.vector
        def _(dve):
            dve.sem_inc(out_taken, RING_O)
            with dve.Fori(0, BATCH) as b:
                dve.wait_ge(gT_done, b + 2)
                dve.tensor_copy(gT[:].rearrange("e q p -> e (q p)"), p_g[0:E, :]).then_inc(gT_ready, 1)
                for s in range(SUMS):
                    last = (E_S + s) * HT
                    if s:
                        dve.wait_ge(acc_ready, b * SUMS + s)
                    dve.wait_ge(w2_done, b * U + last + RING_G)
                    bank = p_o[:, s % RING_O, :].rearrange("p (q c) -> p q c", c=C)
                    if s == 0:
                        ins = dve.tensor_tensor(acc[:], bank, t["u"][:, ds(b * QB, QB), :], ALU.add)
                    else:
                        for q in range(QB):
                            gate = t["gate"][:].rearrange("p q e -> p (q e)")[:, ds(b * (QB * E) + q * E + E_S + s - 1, 1)]
                            ins = dve.scalar_tensor_tensor(out=acc[:, q, :], in0=bank[:, q, :], scalar=gate,
                                                           in1=acc[:, q, :], op0=ALU.mult, op1=ALU.add)
                    ins.then_inc(acc_ready, 1)
                    dve.wait_ge(acc_ready, b * SUMS + s + 1)
                    dve.sem_inc(out_taken, 1)
                dve.wait_ge(stored, b * 16 + 16)
                dve.tensor_tensor(res[:], acc[:], t["modB"][:, 3, ds(b, 1), :].to_broadcast([P, QB, C]),
                                  ALU.mult).then_inc(res_ready, 1)
                dve.wait_ge(res_ready, b * 2 + 1)
                dve.tensor_tensor(res[:], res[:], t["x"][:, ds(b * QB, QB), :], ALU.add).then_inc(res_ready, 1)

        @block.sync
        def _(sp):
            sp.sem_inc(stored, 16)
            out = dram["out"].rearrange("(b q p) c -> b p q c", q=QB, p=P)
            with sp.Fori(0, BATCH) as b:
                sp.wait_ge(res_ready, b * 2 + 2)
                sp.dma_start(out[ds(b, 1)].rearrange("b p q c -> (b p) q c"), res[:]).then_inc(stored, 16)
            sp.wait_ge(stored, 16 * (BATCH + 1))


def program(nc, dram):
    with ExitStack() as ctx:
        t = {}

        def keep(name, shape, dt=F32):
            t[name] = ctx.enter_context(nc.sbuf_tensor("t_" + name, shape, dt))

        keep("ident", [P, P])
        keep("x", [P, QUADS, C])
        keep("hT", [P, QUADS + 2, P])
        keep("modB", [P, 4, BATCH, C])
        for name in ("mean", "var", "rstd"):
            keep(name, [P, QUADS])
        keep("stats", [P, QUADS, 6])
        keep("saT", [P, BATCH])
        keep("caT", [P, BATCH])
        with ExitStack() as first:
            for name in ("wq", "wk"):
                t[name] = first.enter_context(nc.sbuf_tensor("t_" + name, [P, CHUNKS, 2, DH], F32))
            t["wv"] = first.enter_context(nc.sbuf_tensor("t_wv", [P, CHUNKS * DH], F32))
            t["wo"] = first.enter_context(nc.sbuf_tensor("t_wo", [P, CHUNKS, C], F32))
            prepare(nc, t, dram)
            attend(nc, t)
        keep("u", [P, QUADS, C])
        keep("unT", [P, QUADS * P])
        keep("w1", [P, E, HID])
        keep("w2", [P, E, HT, C])
        keep("b1", [P, E * HT])
        keep("b2", [E, C])
        keep("cent", [P, E_R])
        keep("g2", [P, 2])
        keep("gate", [P, QUADS, E])
        route(nc, t, dram)
        mix(nc, t, dram)


def kernel(L0_attn_x, L0_attn_wq, L0_attn_wk, L0_attn_wv, L0_attn_wo, L0_ffn_g_shared, L0_ffn_W1_s, L0_ffn_b1_s,
           L0_ffn_W2_s, L0_ffn_b2_s, L0_ffn_g_routed, L0_ffn_W1_r, L0_ffn_b1_r, L0_ffn_W2_r, L0_ffn_b2_r,
           L0_ffn_centroids, L0_c, L0_wmod):
    import numpy as np
    import concourse.bacc as bacc
    from concourse.bass_utils import run_bass_kernel_spmd

    a = lambda v: np.asarray(v)
    arrays = {
        "x": a(L0_attn_x).reshape(BATCH * SEQ, C),
        "wqT": a(L0_attn_wq).T, "wkT": a(L0_attn_wk).T, "wvT": a(L0_attn_wv).T,
        "woT": a(L0_attn_wo).T.reshape(CHUNKS, DH, C).transpose(1, 0, 2).reshape(DH, CHUNKS * C),
        "cT": a(L0_c).T, "wmod": a(L0_wmod),
        "g2": np.stack([a(L0_ffn_g_shared), a(L0_ffn_g_routed)], axis=1),
        "w1s": a(L0_ffn_W1_s), "w2s": a(L0_ffn_W2_s), "w1r": a(L0_ffn_W1_r), "w2r": a(L0_ffn_W2_r),
        "b1s": a(L0_ffn_b1_s).reshape(E_S * HT, P).T, "b1r": a(L0_ffn_b1_r).reshape(E_R * HT, P).T,
        "b2s": a(L0_ffn_b2_s), "b2r": a(L0_ffn_b2_r), "cent": a(L0_ffn_centroids),
    }
    arrays = {k + "_dram": np.ascontiguousarray(v) for k, v in arrays.items()}
    nc = bacc.Bacc("TRN2", target_bir_lowering=False, num_devices=1)
    dram = {k[:-5]: nc.dram_tensor(k, v.shape, F32, kind="ExternalInput").ap() for k, v in arrays.items()}
    dram["out"] = nc.dram_tensor("out_dram", (BATCH * SEQ, C), F32, kind="ExternalOutput").ap()
    program(nc, dram)
    r = run_bass_kernel_spmd(nc, [arrays], core_ids=[0])
    return r.results[0]["out_dram"].reshape(BATCH, SEQ, C)
```

```python
from contextlib import ExitStack

import concourse.bass as bass
from concourse import mybir

F32 = mybir.dt.float32
F32R = mybir.dt.float32r
ACT = mybir.ActivationFunctionType
ALU = mybir.AluOpType
AX = mybir.AxisListType
ds = bass.ds

P = 128
BATCH, SEQ, C = 8, 512, 128
HEADS, DH = 16, 64
CHUNKS = HEADS
GT = SEQ // HEADS
NPOS = GT * CHUNKS
QUADS = BATCH * SEQ // P
GQ = P // GT
QB = SEQ // P
IT = NPOS // P
KQ = GQ * IT
PAIR = 2
KN = PAIR * KQ
GN = PAIR * GQ
E_S, E_R, HID = 2, 8, 512
E = E_S + E_R
HT = HID // P
EPS_LN = 1e-5
EPS_RMS = float(2.0 ** -23)
NEG = -1.0
TOPK = 2
RING_S, RING_T, RING_P = 2, 2, 4
STEPS = QUADS // PAIR
T_LAG = 3
QK_AT, V_AT = (0, 4, 8, 12), (2, 5, 9, 11)
Y_AT = (13, 15)
PV_LAG = 10
FN, PN = 4 * PAIR, GN // 2
RING_G, RING_O = 4, 3


class Count:

    def __init__(self, eng, n):
        self.eng, self.n = eng, n

    def __call__(self, sem, per, count):
        if isinstance(self.n, int):
            if self.n * per + count > 0:
                self.eng.wait_ge(sem, self.n * per + count)
        else:
            self.eng.wait_ge(sem, self.n * per + count)


def chain(eng, sem):
    seen = [0]

    def link(ins):
        seen[0] += 1
        ins.then_inc(sem, 1)
        eng.wait_ge(sem, seen[0])

    return link


def prepare(nc, t, dram):
    with ExitStack() as ctx:
        sem = lambda name: ctx.enter_context(nc.semaphore(name))
        sb = lambda name, shape, dt=F32: ctx.enter_context(nc.sbuf_tensor(name, shape, dt))
        loaded_x, loaded_c, loaded_w = sem("loaded_x"), sem("loaded_c"), sem("loaded_w")
        ident_ready, exp_c, silu_ready, modT_done, modB_done = map(
            sem, ("ident_ready", "exp_c", "silu_ready", "modT_done", "modB_done"))
        modB_copied, var_ready, std_ready, z_ready, zT_done, hT_ready = map(
            sem, ("modB_copied", "var_ready", "std_ready", "z_ready", "zT_done", "hT_ready"))
        dchain, achain, pchain = sem("dve_chain_a"), sem("act_chain_a"), sem("pool_chain_a")
        cT, sc, ec = sb("cT", [P, BATCH]), sb("sc", [P, BATCH]), sb("ec", [P, BATCH])
        scB = sb("scB", [P, BATCH, P])
        wmod = sb("wmod", [P, 6 * C])
        z = sb("z", [P, 2, QB, C])
        gsign = sb("gsign", [P, BATCH, C])
        pmod = ctx.enter_context(nc.psum_tensor("pmod", [P, 2, 512], F32))
        pT = ctx.enter_context(nc.psum_tensor("pT", [P, 2, 512], F32))
        pm = ctx.enter_context(nc.psum_tensor("pm", [P, 2, BATCH], F32))
        block = ctx.enter_context(nc.Block())

        @block.sync
        def _(sp):
            sp.dma_start(cT[:], dram["cT"]).then_inc(loaded_c, 16)
            sp.dma_start(wmod[:], dram["wmod"]).then_inc(loaded_c, 16)
            sp.dma_start(t["x"][:], dram["x"].rearrange("(q p) c -> p q c", p=P)).then_inc(loaded_x, 16)
            for name in ("wq", "wk", "wv", "wo"):
                sp.dma_start(t[name][:], dram[name + "T"]).then_inc(loaded_w, 16)
            sp.wait_ge(loaded_w, 4 * 16)
            sp.wait_ge(loaded_x, 16)

        @block.gpsimd
        def _(pool):
            link = chain(pool, pchain)
            link(pool.memset(t["ident"][:], 0.0))
            pool.affine_select(out=t["ident"][:], in_=t["ident"][:], compare_op=ALU.not_equal, fill=1.0,
                               base=0, pattern=[[-1, P]], channel_multiplier=1).then_inc(ident_ready, 1)
            link(pool.memset(t["hT"][:, QUADS:QUADS + 2, :], 0.0))

        @block.scalar
        def _(act):
            act.wait_ge(loaded_c, 32)
            act.activation(ec[:], cT[:], ACT.Exp, scale=NEG).then_inc(exp_c, 1)
            for b in range(BATCH):
                act.wait_ge(modB_done, b + 1)
                act.activation(t["modB"][:, :, b, :], pmod[:, b % 2, :].rearrange("p (k c) -> p k c", c=C),
                               ACT.Copy).then_inc(modB_copied, 1)
            act.wait_ge(var_ready, 1)
            act.activation(t["rstd"][:], t["var"][:], ACT.Sqrt).then_inc(std_ready, 1)

        @block.tensor
        def _(pe):
            pe.wait_ge(silu_ready, 1)
            for k in range(2):
                mm = pe.matmul(pm[:, k, :], wmod[:, k * C:(k + 1) * C], sc[:], start=True, stop=True)
            mm.then_inc(modT_done, 1)
            pe.wait_ge(silu_ready, 2)
            for b in range(BATCH):
                if b >= 2:
                    pe.wait_ge(modB_copied, b - 1)
                pe.matmul(pmod[:, b % 2, :], scB[:, b, :], wmod[:, 2 * C:6 * C], start=True,
                          stop=True).then_inc(modB_done, 1)
            pe.wait_ge(ident_ready, 1)
            for b in range(BATCH):
                pe.wait_ge(z_ready, b + 1)
                if b >= 2:
                    pe.wait_ge(hT_ready, b - 1)
                for q in range(QB):
                    mm = pe.transpose(pT[:, b % 2, q * P:(q + 1) * P], z[:, b % 2, q, :], t["ident"][:])
                mm.then_inc(zT_done, 1)

        @block.vector
        def _(dve):
            link = chain(dve, dchain)
            dve.wait_ge(exp_c, 1)
            link(dve.tensor_scalar(ec[:], ec[:], 1.0, None, ALU.add))
            link(dve.reciprocal(ec[:], ec[:]))
            dve.tensor_tensor(sc[:], ec[:], cT[:], ALU.mult).then_inc(silu_ready, 1)
            dve.wait_ge(silu_ready, 1)
            dve.tensor_copy(scB[:], sc[:].unsqueeze(2).to_broadcast([P, BATCH, P])).then_inc(silu_ready, 1)
            dve.wait_ge(loaded_x, 16)
            layernorm_stats(dve, link, t)
            dve.tensor_scalar(t["var"][:], t["var"][:], EPS_LN, None, ALU.add).then_inc(var_ready, 1)
            dve.wait_ge(modT_done, 1)
            link(dve.tensor_copy(t["saT"][:], pm[:, 0, :]))
            link(dve.tensor_scalar(t["caT"][:], pm[:, 1, :], 1.0, None, ALU.add))
            dve.wait_ge(std_ready, 1)
            link(dve.reciprocal(t["rstd"][:], t["rstd"][:]))
            for b in range(BATCH + 1):
                if b < BATCH:
                    if b >= 2:
                        dve.wait_ge(zT_done, b - 1)
                    for q in range(QB):
                        k = b * QB + q
                        ins = dve.tensor_scalar(z[:, b % 2, q, :], t["x"][:, k, :], t["mean"][:, k:k + 1],
                                                t["rstd"][:, k:k + 1], ALU.subtract, ALU.mult)
                    ins.then_inc(z_ready, 1)
                if b >= 1:
                    dve.wait_ge(zT_done, b)
                    dve.tensor_scalar(t["hT"][:, (b - 1) * QB:b * QB, :].rearrange("p q c -> p (q c)"),
                                      pT[:, (b - 1) % 2, :], t["caT"][:, b - 1:b], t["saT"][:, b - 1:b],
                                      ALU.mult, ALU.add).then_inc(hT_ready, 1)
            dve.wait_ge(loaded_w, 4 * 16)
            link(dve.tensor_scalar(t["wq"][:], t["wq"][:], float(DH) ** -0.5, None, ALU.mult))
            dve.wait_ge(modB_copied, BATCH)
            for k in (0, 3):
                g = t["modB"][:, k, :, :]
                link(dve.tensor_scalar(gsign[:], g, 0.0, 2.0, ALU.is_ge, ALU.mult))
                link(dve.tensor_scalar(gsign[:], gsign[:], -1.0, None, ALU.add))
                link(dve.tensor_tensor(g, g, gsign[:], ALU.mult))
                link(dve.tensor_scalar(g, g, 0.25, None, ALU.max))
                link(dve.tensor_tensor(g, g, gsign[:], ALU.mult))
            link(dve.tensor_scalar(t["modB"][:, 2, :, :], t["modB"][:, 2, :, :], 1.0, None, ALU.add))


def layernorm_stats(dve, link, t):
    st = t["stats"]
    for q in range(QUADS):
        ins = dve.bn_stats(st[:, q, :], t["x"][:, q, :])
    link(ins)
    me, m2e, mo, m2o = (st[:, :, k] for k in (1, 2, 4, 5))
    link(dve.tensor_tensor(t["mean"][:], me, mo, ALU.add))
    link(dve.tensor_tensor(t["var"][:], me, mo, ALU.subtract))
    link(dve.tensor_scalar(t["mean"][:], t["mean"][:], 0.5, None, ALU.mult))
    link(dve.scalar_tensor_tensor(out=t["var"][:], in0=t["var"][:], scalar=C / 4.0, in1=t["var"][:],
                                  op0=ALU.mult, op1=ALU.mult))
    link(dve.tensor_tensor(t["var"][:], t["var"][:], m2e, ALU.add))
    link(dve.tensor_tensor(t["var"][:], t["var"][:], m2o, ALU.add))
    link(dve.tensor_scalar(t["var"][:], t["var"][:], 1.0 / C, None, ALU.mult))


def attend(nc, t):
    with ExitStack() as ctx:
        sem = lambda name: ctx.enter_context(nc.semaphore(name))
        sb = lambda name, shape, dt=F32: ctx.enter_context(nc.sbuf_tensor(name, shape, dt))
        psum = lambda name, n: ctx.enter_context(nc.psum_tensor(name, [P, n, 512], F32))
        hq_ready, y_done, y_out = sem("hq_ready"), sem("y_done"), sem("y_out")
        qk_done, part_hi, part_lo, k_copied = sem("qk_done"), sem("part_hi"), sem("part_lo"), sem("k_copied")
        v_done, v_ready = sem("v_done"), sem("v_ready")
        pv_done, o_dve, o_act = sem("pv_done"), sem("o_dve"), sem("o_act")
        s_done, max_done, exp_done, rden_done, p_scaled, t_done, t_out = map(
            sem, ("s_done", "max_done", "exp_done", "rden_done", "p_scaled", "t_done", "t_out"))
        pool_turn = sem("pool_turn")

        hq = sb("hq", [P, 2, P])
        Q = sb("Q", [P, 2, GQ, NPOS], F32R)
        KH = sb("KH", [P, 2, GQ, NPOS], F32R)
        KL = sb("KL", [P, 2, GQ, NPOS], F32R)
        V = sb("V", [P, 2, GQ, IT, DH])
        prob = sb("prob", [P, RING_P, NPOS])
        PT = sb("PT", [P, GQ, IT, NPOS])
        O = sb("O", [P, CHUNKS // 2, P])
        nmax, den, rden = (sb(name, [P, RING_P]) for name in ("nmax", "den", "rden"))
        ps_s, ps_t, ps_o, ps_qk, ps_vy = (
            psum("ps_s", RING_S), psum("ps_t", RING_T), psum("ps_o", 2), psum("ps_qk", 1), psum("ps_vy", 1))
        ps_v, ps_y = ps_vy[:, 0, 0:IT * DH], ps_vy[:, 0, IT * DH:IT * DH + C]
        hT, ident = t["hT"], t["ident"]
        HALF = (slice(0, DH), slice(DH, P))

        def within(n, per, index):
            return not isinstance(n, int) or 0 <= n * per + index < STEPS * per

        def fill_of(k):
            return 4 * (k // KQ + 1) + QK_AT.index(k % KQ)

        def project(pe, n, k):
            cnt, quad, kq = Count(pe, n), k // KQ, k % KQ
            nxt = 1 - quad
            if kq in QK_AT:
                f = QK_AT.index(kq)
                w, half = (t["wk"], t["wq"])[f % 2], f // 2
                cnt(part_lo, FN * 2, 2 * fill_of(k))
                if f == 0:
                    cnt(hq_ready, PAIR, quad + 2)
                for c in range(4):
                    pair = 4 * half + c
                    mm = pe.matmul(ps_qk[:, 0, c * P:(c + 1) * P], w[:, pair * P:(pair + 1) * P], hq[:, nxt, :],
                                   start=True, stop=True)
                mm.then_inc(qk_done, 1)
            if kq in V_AT:
                slot = V_AT.index(kq)
                cnt(v_ready, GN, GQ * (quad + 1) + slot)
                cnt(y_out, PAIR, quad - 1)
                wv = t["wv"][:].rearrange("p (a c d) -> p c a d", c=4, d=DH)
                for c in range(4):
                    mm = pe.matmul(ps_v[c * GT:(c + 1) * GT, :],
                                   hq[:, nxt, slot * GT:(slot + 1) * GT], wv[:, c], start=True, stop=True,
                                   tile_position=(0, c * GT))
                mm.then_inc(v_done, 1)

        def pe_tile(pe, n, k):
            cnt, kq = Count(pe, n), k % KQ
            if within(n, KN, k):
                par, slot, i = (k // KQ) % 2, kq // IT, k % IT
                if kq == 0:
                    cnt(part_lo, FN * 2, 8 * (k // KQ + 1))
                    cnt(k_copied, 64 * PAIR, 64 * (k // KQ + 1))
                cnt(exp_done, KN, k - RING_S + 1)
                for part in (KH, KL):
                    mm = pe.matmul(ps_s[:, k % RING_S, :], Q[:, par, slot, i * P:(i + 1) * P],
                                   part[:, par, slot, :], start=(part is KH), stop=(part is KL))
                mm.then_inc(s_done, 1)
                project(pe, n, k)
            kt = k - T_LAG
            if within(n, KN, kt):
                cnt(p_scaled, KN, kt + 1)
                cnt(t_out, KN, kt - RING_T + 1)
                for a in range(IT):
                    mm = pe.transpose(ps_t[:, kt % RING_T, a * P:(a + 1) * P],
                                      prob[:, kt % RING_P, a * P:(a + 1) * P], ident[:])
                mm.then_inc(t_done, 1)
            p, j = (k - PV_LAG) // 8, (k - PV_LAG) % 8
            if within(n, PN, p):
                half, a = j // IT, j % IT
                cols = slice(half * 256, half * 256 + 256)
                if a == 0:
                    cnt(t_out, KN, 8 * p + IT + 2 * (half + 1))
                if j == 0:
                    cnt(v_ready, GN, 2 * (p + 1))
                    cnt(o_dve, 2 * PN, 2 * (p - 1))
                    cnt(o_act, 2 * PN, 2 * (p - 1))
                for m in range(2):
                    g = 2 * p + m
                    mm = pe.matmul(ps_o[HALF[m], p % 2, cols], V[:, (g // GQ) % 2, g % GQ, a, :],
                                   PT[:, g % GQ, a, cols], start=(j == 0), stop=(a == IT - 1),
                                   tile_position=(0, m * DH), skip_group_check=True)
                if j == 7:
                    mm.then_inc(pv_done, 1)
            qt = k // KQ - 1
            if kq in Y_AT and within(n, PAIR, qt):
                if kq == Y_AT[0]:
                    cnt(o_dve, 2 * PN, 4 * (qt + 1))
                    cnt(o_act, 2 * PN, 4 * (qt + 1))
                    cnt(v_ready, GN, GQ * (qt + (3 if within(n, KN, k) else 2)))
                y_part = Y_AT.index(kq)
                for c in range(4 * y_part, 4 * y_part + 4):
                    mm = pe.matmul(ps_y, O[:, c, :], t["wo"][:, c * C:(c + 1) * C], start=(c == 0),
                                   stop=(c == CHUNKS // 2 - 1), skip_group_check=True)
                if y_part:
                    mm.then_inc(y_done, 1)

        def by_group(rows):
            return ps_qk[rows, 0, :].rearrange("p (c g t) -> p c g t", c=4, g=GQ)

        def into_groups(buf, rows, par, half, odd):
            v = buf[rows, par, :, :].rearrange("p g (c o t) -> p o c g t", o=2, t=GT)
            return v[:, odd, 4 * half:4 * half + 4]

        def o_half(m, p, odd):
            slot = (2 * p + m) % GQ
            return (O[HALF[odd], :, slot * GT:(slot + 1) * GT],
                    ps_o[HALF[m], p % 2, :].rearrange("p (c o t) -> p o c t", o=2, t=GT)[:, odd])

        def before_o(cnt, p, odd):
            if odd == 0:
                cnt(pv_done, PN, p + 1)
                if p % 2 == 0:
                    cnt(y_done, PAIR, p // 2)

        def act_project(act, n, k):
            cnt = Count(act, n)
            for odd in range(2):
                if (k - odd) % KQ in QK_AT:
                    ks = k - odd
                    f = QK_AT.index(ks % KQ)
                    cnt(qk_done, FN, fill_of(ks) + 1)
                    act.activation(into_groups((KH, Q)[f % 2], HALF[0], 1 - ks // KQ, f // 2, odd),
                                   by_group(HALF[odd]), ACT.Copy).then_inc(part_hi, 1)

        def act_tile(act, n, k):
            cnt = Count(act, n)
            if within(n, KN, k):
                cnt(max_done, KN, k + 1)
                cnt(t_done, KN, k - RING_P + 1)
                r = k % RING_P
                act.activation(prob[:, r, :], ps_s[:, k % RING_S, :], ACT.Exp, bias=nmax[:, r:r + 1],
                               accum_out=den[:, r:r + 1]).then_inc(exp_done, 1)
                act_project(act, n, k)
            kt = k - T_LAG
            if within(n, KN, kt):
                gt, it = kt // IT, kt % IT
                cnt(t_done, KN, kt + 1)
                if it == 0:
                    cnt(pv_done, PN, gt // 2 - 1)
                act.activation(PT[:, gt % GQ, :, it * P:(it + 1) * P],
                               ps_t[:, kt % RING_T, :].rearrange("p (a q) -> p a q", a=IT),
                               ACT.Copy).then_inc(t_out, 1)
            p, odd = (k - PV_LAG) // 8 - 1, (k - PV_LAG) % 8
            if odd < 2 and within(n, PN, p):
                before_o(cnt, p, odd)
                o, sums = o_half(1, p, odd)
                act.activation(o, sums, ACT.Copy).then_inc(o_act, 1)
            qt = k // KQ - 2
            if k % KQ == 0 and within(n, PAIR, qt):
                cnt(y_done, PAIR, qt + 1)
                act.activation(hT[:, ds(n * PAIR + qt, 1), :].rearrange("p q c -> p (q c)"), ps_y,
                               ACT.Copy).then_inc(y_out, 1)

        def dve_project(dve, n, k):
            cnt, quad, kq = Count(dve, n), k // KQ, k % KQ
            for late in (1, 2):
                if (k - late) % KQ in QK_AT:
                    ks, odd = k - late, late - 1
                    f = QK_AT.index(ks % KQ)
                    par, half = 1 - ks // KQ, f // 2
                    cnt(part_hi, 2 * FN, 2 * fill_of(ks) + odd + 1)
                    hi, lo = ((KH, KL), (Q, Q))[f % 2]
                    dve.tensor_tensor(into_groups(lo, HALF[f % 2], par, half, odd), by_group(HALF[odd]),
                                      into_groups(hi, HALF[0], par, half, odd), ALU.subtract).then_inc(part_lo, 1)
            if kq in V_AT:
                slot = V_AT.index(kq)
                cnt(v_done, GN, GQ * (quad + 1) + slot + 1)
                cnt(pv_done, PN, 2 * (quad - 1) + slot // 2 + 1)
                dve.tensor_copy(V[:, 1 - quad, slot, :, :], ps_v.rearrange("p (a d) -> p a d", d=DH)
                                ).then_inc(v_ready, 1)

        def dve_tile(dve, n, k):
            cnt = Count(dve, n)
            r = k % RING_P
            if within(n, KN, k):
                cnt(s_done, KN, k + 1)
                dve.tensor_reduce(nmax[:, r:r + 1], ps_s[:, k % RING_S, :], AX.X, ALU.max,
                                  negate=True).then_inc(max_done, 1)
            p, odd = (k - PV_LAG) // 8 - 1, (k - PV_LAG) % 8
            if odd < 2 and within(n, PN, p):
                before_o(cnt, p, odd)
                o, sums = o_half(0, p, odd)
                dve.tensor_copy(o, sums).then_inc(o_dve, 1)
            if within(n, KN, k):
                cnt(exp_done, KN, k + 1)
                dve.reciprocal(rden[:, r:r + 1], den[:, r:r + 1]).then_inc(rden_done, 1)
                dve_project(dve, n, k)

        def pool_tile(pool, n, k):
            cnt, r = Count(pool, n), k % RING_P
            cnt(rden_done, KN, k + 1)
            pool.sem_inc(pool_turn, 1)
            pool.tensor_scalar(prob[:, r, :], prob[:, r, :], rden[:, r:r + 1], 1.0, ALU.mult,
                               ALU.mult).then_inc(p_scaled, 1)
            if k % KQ == 1:
                quad = k // KQ
                cnt(qk_done, FN, 4 * (quad + 1))
                pool.tensor_copy(hq[:, quad, :], hT[:, ds(n * PAIR + quad + 2, 1), :].rearrange("p q c -> p (q c)")
                                 ).then_inc(hq_ready, 1)

        def copy_keys(sp, n, quad):
            cnt, nxt = Count(sp, n), 1 - quad
            for half in range(2):
                for buf, ready in ((KH, part_hi), (KL, part_lo)):
                    cnt(ready, 2 * FN, 2 * (4 * (quad + 1) + 2 * half + 1))
                    cols = slice(8 * half * GT, 8 * (half + 1) * GT)
                    sp.dma_start(buf[HALF[1], nxt, :, cols].bitcast(F32),
                                 buf[HALF[0], nxt, :, cols].bitcast(F32)).then_inc(k_copied, 16)

        def steps(eng, tile):
            for k in range(KN):
                tile(eng, 0, k)
            with eng.Fori(1, STEPS) as n:
                for k in range(KN):
                    tile(eng, n, k)

        block = ctx.enter_context(nc.Block())

        @block.sync
        def _(sp):
            copy_keys(sp, -1, 1)
            with sp.Fori(0, STEPS) as n:
                for quad in range(PAIR):
                    copy_keys(sp, n, quad)
            sp.wait_ge(k_copied, 64 * (QUADS + 1))

        @block.tensor
        def _(pe):
            for k in range(KQ, KN):
                project(pe, -1, k)
            steps(pe, pe_tile)
            for k in range(KQ + 1):
                pe_tile(pe, STEPS, k)

        @block.scalar
        def _(act):
            for k in range(KQ, KN):
                act_project(act, -1, k)
            steps(act, act_tile)
            for k in range(KQ + 1):
                act_tile(act, STEPS, k)

        @block.vector
        def _(dve):
            for k in range(KQ, KN):
                dve_project(dve, -1, k)
            steps(dve, dve_tile)
            for k in range(KQ + 1):
                dve_tile(dve, STEPS, k)

        @block.gpsimd
        def _(pool):
            for quad in range(2):
                pool.tensor_copy(hq[:, quad, :], hT[:, quad, :]).then_inc(hq_ready, 1)
            steps(pool, pool_tile)


def route(nc, t, dram):
    with ExitStack() as ctx:
        sem = lambda name: ctx.enter_context(nc.semaphore(name))
        sb = lambda name, shape, dt=F32: ctx.enter_context(nc.sbuf_tensor(name, shape, dt))
        (w1_loaded, w_loaded, lower_ready, var_ready, std_ready, u_ready, ms_ready, mse_ready, rms_ready, un_ready,
         tr_done, uT_ready, unT_ready, logit_done, logit_ready, expl) = map(
            sem, ("w1_loaded", "w_loaded", "lower_ready", "var_ready2", "std_ready2", "u_ready", "ms_ready", "mse_ready",
                  "rms_ready", "un_ready", "tr_done", "uT_ready", "unT_ready", "logit_done", "logit_ready", "expl"))
        dchain, pchain = sem("dve_chain_c"), sem("pool_chain_c")
        z = sb("z2", [P, 2, QB, C])
        sq = sb("sq", [P, 2, C])
        un = sb("un", [P, 2, QB, C])
        ms, rr = sb("ms", [P, QUADS]), sb("rr", [P, QUADS])
        uT = sb("uT", [P, 2, 512])
        logit = sb("logit", [P, QUADS, E_R])
        lower = sb("lower", [P, E_R, E_R])
        gt_, eq = sb("gt_", [P, QUADS, E_R, E_R]), sb("eq", [P, QUADS, E_R, E_R])
        rank, ssum = sb("rank", [P, QUADS, E_R]), sb("ssum", [P, QUADS])
        p_u = ctx.enter_context(nc.psum_tensor("p_u", [P, 2, 512], F32))
        p_n = ctx.enter_context(nc.psum_tensor("p_n", [P, 2, 512], F32))
        p_l = ctx.enter_context(nc.psum_tensor("p_l", [P, 2, 512], F32))
        block = ctx.enter_context(nc.Block())
        x, y = t["x"], t["hT"]

        @block.sync
        def _(sp):
            for name in ("cent", "g2"):
                sp.dma_start(t[name][:], dram[name]).then_inc(w_loaded, 16)
            for e in range(E_S):
                sp.dma_start(t["w1"][:, e, :], dram["w1s"][e]).then_inc(w1_loaded, 16)
                sp.dma_start(t["w2"][:, e, :, :], dram["w2s"][e].rearrange("(h p) c -> p h c", p=P)).then_inc(w_loaded, 16)
            for e in range(E_R):
                sp.dma_start(t["w1"][:, E_S + e, :], dram["w1r"][e]).then_inc(w1_loaded, 16)
                sp.dma_start(t["w2"][:, E_S + e, :, :], dram["w2r"][e].rearrange("(h p) c -> p h c", p=P)).then_inc(w_loaded, 16)
            sp.dma_start(t["b1"][:, 0:E_S * HT], dram["b1s"]).then_inc(w_loaded, 16)
            sp.dma_start(t["b1"][:, E_S * HT:], dram["b1r"]).then_inc(w_loaded, 16)
            sp.dma_start(t["b2"][0:E_S, :], dram["b2s"]).then_inc(w_loaded, 16)
            sp.dma_start(t["b2"][E_S:E, :], dram["b2r"]).then_inc(w_loaded, 16)
            sp.wait_ge(w_loaded, 16 * (6 + E))

        @block.gpsimd
        def _(pool):
            link = chain(pool, pchain)
            link(pool.memset(lower[:], 1.0))
            pool.affine_select(out=lower[:], in_=lower[:], compare_op=ALU.is_gt, fill=0.0, base=0,
                               pattern=[[1, E_R], [-1, E_R]], channel_multiplier=0).then_inc(lower_ready, 1)

        @block.scalar
        def _(act):
            act.wait_ge(var_ready, 1)
            act.activation(t["rstd"][:], t["var"][:], ACT.Sqrt).then_inc(std_ready, 1)
            for k in range(QUADS):
                if k % QB == 0:
                    act.wait_ge(u_ready, k // QB + 1)
                if k >= 2:
                    act.wait_ge(ms_ready, k - 1)
                act.activation(sq[:, k % 2, :], t["u"][:, k, :], ACT.Square, accum_out=ms[:, k:k + 1]).then_inc(ms_ready, 1)
            act.wait_ge(mse_ready, 1)
            act.activation(rr[:], rr[:], ACT.Sqrt).then_inc(rms_ready, 1)
            for b in range(BATCH + 1):
                if b < BATCH:
                    act.wait_ge(tr_done, b + 1)
                    if b >= 2:
                        act.wait_ge(logit_done, b - 1)
                    act.activation(uT[:, b % 2, :], p_u[:, b % 2, :], ACT.Copy).then_inc(uT_ready, 1)
                if b >= 1:
                    act.wait_ge(logit_done, b)
                    act.activation(logit[:, (b - 1) * QB:b * QB, :],
                                   p_l[:, (b - 1) % 2, 0:QB * E_R].rearrange("p (q e) -> p q e", e=E_R),
                                   ACT.Copy).then_inc(logit_ready, 1)
            act.wait_ge(logit_ready, BATCH)
            act.activation(logit[:], logit[:], ACT.Exp, scale=NEG).then_inc(expl, 1)

        @block.tensor
        def _(pe):
            pe.wait_ge(w_loaded, 16 * (6 + E))
            for b in range(BATCH + 1):
                if b < BATCH:
                    pe.wait_ge(un_ready, b + 1)
                    if b >= 2:
                        pe.wait_ge(uT_ready, b - 1)
                        pe.wait_ge(unT_ready, b - 1)
                    for q in range(QB):
                        pe.transpose(p_u[:, b % 2, q * P:(q + 1) * P], t["u"][:, b * QB + q, :], t["ident"][:])
                        mm = pe.transpose(p_n[:, b % 2, q * P:(q + 1) * P], un[:, b % 2, q, :], t["ident"][:])
                    mm.then_inc(tr_done, 1)
                if b >= 1:
                    pe.wait_ge(uT_ready, b)
                    if b >= 3:
                        pe.wait_ge(logit_ready, b - 2)
                    for q in range(QB):
                        mm = pe.matmul(p_l[:, (b - 1) % 2, q * E_R:(q + 1) * E_R], uT[:, (b - 1) % 2, q * P:(q + 1) * P],
                                       t["cent"][:], start=True, stop=True)
                    mm.then_inc(logit_done, 1)

        @block.vector
        def _(dve):
            link = chain(dve, dchain)

            def spread(k, b):
                return t["modB"][:, k, b, :].unsqueeze(1).to_broadcast([P, QB, C])

            for b in range(BATCH):
                yb = y[:, b * QB:(b + 1) * QB, :]
                ins = dve.tensor_tensor(yb, yb, spread(0, b), ALU.mult)
            link(ins)
            for b in range(BATCH):
                sl = slice(b * QB, (b + 1) * QB)
                ins = dve.tensor_tensor(x[:, sl, :], x[:, sl, :], y[:, sl, :], ALU.add)
            link(ins)
            layernorm_stats(dve, link, t)
            dve.tensor_scalar(t["var"][:], t["var"][:], EPS_LN, None, ALU.add).then_inc(var_ready, 1)
            dve.wait_ge(std_ready, 1)
            link(dve.reciprocal(t["rstd"][:], t["rstd"][:]))
            for b in range(BATCH):
                sl = slice(b * QB, (b + 1) * QB)
                for k in range(b * QB, (b + 1) * QB):
                    ins = dve.tensor_scalar(z[:, b % 2, k % QB, :], x[:, k, :], t["mean"][:, k:k + 1],
                                            t["rstd"][:, k:k + 1], ALU.subtract, ALU.mult)
                link(ins)
                link(dve.tensor_tensor(t["u"][:, sl, :], z[:, b % 2, :, :], spread(2, b), ALU.mult))
                dve.tensor_tensor(t["u"][:, sl, :], t["u"][:, sl, :], spread(1, b), ALU.add).then_inc(u_ready, 1)
            dve.wait_ge(ms_ready, QUADS)
            dve.tensor_scalar(rr[:], ms[:], 1.0 / C, EPS_RMS, ALU.mult, ALU.add).then_inc(mse_ready, 1)
            dve.wait_ge(rms_ready, 1)
            link(dve.reciprocal(rr[:], rr[:]))
            for b in range(BATCH + 1):
                if b < BATCH:
                    if b >= 2:
                        dve.wait_ge(tr_done, b - 1)
                    for k in range(b * QB, (b + 1) * QB):
                        ins = dve.tensor_scalar(un[:, b % 2, k % QB, :], t["u"][:, k, :], rr[:, k:k + 1], None, ALU.mult)
                    ins.then_inc(un_ready, 1)
                if b >= 1:
                    dve.wait_ge(tr_done, b)
                    dve.tensor_copy(t["unT"][:, (b - 1) * 512:b * 512], p_n[:, (b - 1) % 2, :]).then_inc(unT_ready, 1)
            dve.wait_ge(w1_loaded, 16 * E)
            dve.wait_ge(w_loaded, 16 * (6 + E))
            link(dve.tensor_scalar(t["w1"][:, 0:E_S, :], t["w1"][:, 0:E_S, :], t["g2"][:, 0:1], None, ALU.mult))
            link(dve.tensor_scalar(t["w1"][:, E_S:E, :], t["w1"][:, E_S:E, :], t["g2"][:, 1:2], None, ALU.mult))
            dve.wait_ge(expl, 1)
            score = logit
            link(dve.tensor_scalar(score[:], score[:], 1.0, None, ALU.add))
            link(dve.reciprocal(score[:], score[:]))
            link(dve.tensor_reduce(ssum[:], score[:], AX.X, ALU.add))
            link(dve.reciprocal(ssum[:], ssum[:]))
            this = score[:].unsqueeze(3).to_broadcast([P, QUADS, E_R, E_R])
            other = score[:].unsqueeze(2).to_broadcast([P, QUADS, E_R, E_R])
            link(dve.tensor_tensor(gt_[:], other, this, ALU.is_gt))
            link(dve.tensor_tensor(eq[:], other, this, ALU.is_equal))
            dve.wait_ge(lower_ready, 1)
            flat = "p e f -> p (e f)"
            link(dve.tensor_tensor(eq[:].rearrange("p q e f -> p q (e f)"), eq[:].rearrange("p q e f -> p q (e f)"),
                                   lower[:].rearrange(flat).unsqueeze(1).to_broadcast([P, QUADS, E_R * E_R]), ALU.mult))
            link(dve.tensor_tensor(gt_[:], gt_[:], eq[:], ALU.add))
            link(dve.tensor_reduce(rank[:], gt_[:], AX.X, ALU.add))
            link(dve.scalar_tensor_tensor(out=rank[:], in0=rank[:], scalar=TOPK - 0.5, in1=score[:], op0=ALU.is_lt,
                                          op1=ALU.mult))
            link(dve.memset(t["gate"][:, :, 0:E_S], 1.0))
            link(dve.tensor_tensor(t["gate"][:, :, E_S:E], rank[:], ssum[:].unsqueeze(2).to_broadcast([P, QUADS, E_R]),
                                   ALU.mult))


def mix(nc, t, dram):
    with ExitStack() as ctx:
        sem = lambda name: ctx.enter_context(nc.semaphore(name))
        sb = lambda name, shape, dt=F32: ctx.enter_context(nc.sbuf_tensor(name, shape, dt))
        h_done, g_ready, w2_done, out_taken, gq_ready, gT_done, gT_ready, acc_ready, res_ready, stored = map(
            sem, ("h_done", "g_ready", "w2_done", "out_taken", "gq_ready", "gT_done", "gT_ready", "acc_ready",
                  "res_ready", "stored"))
        G = sb("G", [P, RING_G, 512])
        acc = sb("acc", [P, QB, C])
        res = sb("res", [P, QB, C])
        gq = sb("gq", [P, QB, E])
        gT = sb("gT", [E, QB, P])
        p_h = ctx.enter_context(nc.psum_tensor("p_h", [P, RING_G, 512], F32))
        p_o = ctx.enter_context(nc.psum_tensor("p_o", [P, RING_O, 512], F32))
        p_g = ctx.enter_context(nc.psum_tensor("p_g", [P, 512], F32))
        block = ctx.enter_context(nc.Block())
        units = [(e, h) for e in range(E) for h in range(HT)]
        U = len(units)
        SUMS = 1 + E_R
        sum_of = lambda e: max(0, e - E_S + 1)
        closes = lambda u: units[u][1] == HT - 1 and units[u][0] >= E_S - 1

        @block.gpsimd
        def _(pool):
            with pool.Fori(0, BATCH) as b:
                pool.wait_ge(gT_done, b + 1)
                pool.tensor_copy(gq[:], t["gate"][:, ds(b * QB, QB), :]).then_inc(gq_ready, 1)

        @block.tensor
        def _(pe):
            pe.sem_inc(w2_done, RING_G)
            pe.sem_inc(gT_done, 1)
            with pe.Fori(0, BATCH) as b:
                pe.wait_ge(gq_ready, b + 1)
                for q in range(QB):
                    mm = pe.transpose(p_g[0:E, q * P:(q + 1) * P], gq[:, q, :], t["ident"][:])
                mm.then_inc(gT_done, 1)

                def second(u):
                    e, h = units[u]
                    s = sum_of(e)
                    first = h == 0 and e in (0, *range(E_S, E))
                    if first:
                        pe.wait_ge(out_taken, b * SUMS + s + 1)
                    if u == 0:
                        pe.wait_ge(gT_ready, b + 1)
                        for q in range(QB):
                            pe.matmul(p_o[:, s % RING_O, q * P:(q + 1) * P], gT[:, q, :], t["b2"][:], start=(q == 0),
                                      stop=False, skip_group_check=True)
                    pe.wait_ge(g_ready, b * U + u + 1)
                    for q in range(QB):
                        mm = pe.matmul(p_o[:, s % RING_O, q * P:(q + 1) * P], G[:, u % RING_G, q * P:(q + 1) * P],
                                       t["w2"][:, e, h, :], start=(first and q == 0 and u > 0), stop=closes(u),
                                       skip_group_check=True)
                    mm.then_inc(w2_done, 1)

                for u in range(U + 1):
                    if u < U:
                        e, h = units[u]
                        pe.matmul(p_h[:, u % RING_G, :], t["w1"][:, e, h * P:(h + 1) * P],
                                  t["unT"][:, ds(b * 512, 512)], start=True, stop=True).then_inc(h_done, 1)
                    if u >= 1:
                        second(u - 1)

        @block.scalar
        def _(act):
            with act.Fori(0, BATCH) as b:
                for u in range(U):
                    act.wait_ge(w2_done, b * U + u + 1)
                    act.wait_ge(h_done, b * U + u + 1)
                    act.activation(G[:, u % RING_G, :], p_h[:, u % RING_G, :], ACT.Gelu,
                                   bias=t["b1"][:, u:u + 1]).then_inc(g_ready, 1)

        @block.vector
        def _(dve):
            dve.sem_inc(out_taken, RING_O)
            with dve.Fori(0, BATCH) as b:
                dve.wait_ge(gT_done, b + 2)
                dve.tensor_copy(gT[:].rearrange("e q p -> e (q p)"), p_g[0:E, :]).then_inc(gT_ready, 1)
                for s in range(SUMS):
                    last = (E_S + s) * HT
                    if s:
                        dve.wait_ge(acc_ready, b * SUMS + s)
                    dve.wait_ge(w2_done, b * U + last + RING_G)
                    bank = p_o[:, s % RING_O, :].rearrange("p (q c) -> p q c", c=C)
                    if s == 0:
                        ins = dve.tensor_tensor(acc[:], bank, t["u"][:, ds(b * QB, QB), :], ALU.add)
                    else:
                        for q in range(QB):
                            gate = t["gate"][:].rearrange("p q e -> p (q e)")[:, ds(b * (QB * E) + q * E + E_S + s - 1, 1)]
                            ins = dve.scalar_tensor_tensor(out=acc[:, q, :], in0=bank[:, q, :], scalar=gate,
                                                           in1=acc[:, q, :], op0=ALU.mult, op1=ALU.add)
                    ins.then_inc(acc_ready, 1)
                    dve.wait_ge(acc_ready, b * SUMS + s + 1)
                    dve.sem_inc(out_taken, 1)
                dve.wait_ge(stored, b * 16 + 16)
                dve.tensor_tensor(res[:], acc[:], t["modB"][:, 3, ds(b, 1), :].to_broadcast([P, QB, C]),
                                  ALU.mult).then_inc(res_ready, 1)
                dve.wait_ge(res_ready, b * 2 + 1)
                dve.tensor_tensor(res[:], res[:], t["x"][:, ds(b * QB, QB), :], ALU.add).then_inc(res_ready, 1)

        @block.sync
        def _(sp):
            sp.sem_inc(stored, 16)
            out = dram["out"].rearrange("(b q p) c -> b p q c", q=QB, p=P)
            with sp.Fori(0, BATCH) as b:
                sp.wait_ge(res_ready, b * 2 + 2)
                sp.dma_start(out[ds(b, 1)].rearrange("b p q c -> (b p) q c"), res[:]).then_inc(stored, 16)
            sp.wait_ge(stored, 16 * (BATCH + 1))


def program(nc, dram):
    with ExitStack() as ctx:
        t = {}

        def keep(name, shape, dt=F32):
            t[name] = ctx.enter_context(nc.sbuf_tensor("t_" + name, shape, dt))

        keep("ident", [P, P])
        keep("x", [P, QUADS, C])
        keep("hT", [P, QUADS + 2, P])
        keep("modB", [P, 4, BATCH, C])
        for name in ("mean", "var", "rstd"):
            keep(name, [P, QUADS])
        keep("stats", [P, QUADS, 6])
        keep("saT", [P, BATCH])
        keep("caT", [P, BATCH])
        with ExitStack() as first:
            for name in ("wq", "wk", "wv", "wo"):
                t[name] = first.enter_context(nc.sbuf_tensor("t_" + name, [P, CHUNKS * DH], F32))
            prepare(nc, t, dram)
            attend(nc, t)
        keep("u", [P, QUADS, C])
        keep("unT", [P, QUADS * P])
        keep("w1", [P, E, HID])
        keep("w2", [P, E, HT, C])
        keep("b1", [P, E * HT])
        keep("b2", [E, C])
        keep("cent", [P, E_R])
        keep("g2", [P, 2])
        keep("gate", [P, QUADS, E])
        route(nc, t, dram)
        mix(nc, t, dram)


def kernel(L0_attn_x, L0_attn_wq, L0_attn_wk, L0_attn_wv, L0_attn_wo, L0_ffn_g_shared, L0_ffn_W1_s, L0_ffn_b1_s,
           L0_ffn_W2_s, L0_ffn_b2_s, L0_ffn_g_routed, L0_ffn_W1_r, L0_ffn_b1_r, L0_ffn_W2_r, L0_ffn_b2_r,
           L0_ffn_centroids, L0_c, L0_wmod):
    import numpy as np
    import concourse.bacc as bacc
    from concourse.bass_utils import run_bass_kernel_spmd

    a = lambda v: np.asarray(v)
    arrays = {
        "x": a(L0_attn_x).reshape(BATCH * SEQ, C),
        "wqT": a(L0_attn_wq).T, "wkT": a(L0_attn_wk).T, "wvT": a(L0_attn_wv).T,
        "woT": a(L0_attn_wo).T.reshape(CHUNKS // 2, P, C).transpose(1, 0, 2).reshape(P, CHUNKS // 2 * C),
        "cT": a(L0_c).T, "wmod": a(L0_wmod),
        "g2": np.stack([a(L0_ffn_g_shared), a(L0_ffn_g_routed)], axis=1),
        "w1s": a(L0_ffn_W1_s), "w2s": a(L0_ffn_W2_s), "w1r": a(L0_ffn_W1_r), "w2r": a(L0_ffn_W2_r),
        "b1s": a(L0_ffn_b1_s).reshape(E_S * HT, P).T, "b1r": a(L0_ffn_b1_r).reshape(E_R * HT, P).T,
        "b2s": a(L0_ffn_b2_s), "b2r": a(L0_ffn_b2_r), "cent": a(L0_ffn_centroids),
    }
    arrays = {k + "_dram": np.ascontiguousarray(v) for k, v in arrays.items()}
    nc = bacc.Bacc("TRN2", target_bir_lowering=False, num_devices=1)
    dram = {k[:-5]: nc.dram_tensor(k, v.shape, F32, kind="ExternalInput").ap() for k, v in arrays.items()}
    dram["out"] = nc.dram_tensor("out_dram", (BATCH * SEQ, C), F32, kind="ExternalOutput").ap()
    program(nc, dram)
    r = run_bass_kernel_spmd(nc, [arrays], core_ids=[0])
    return r.results[0]["out_dram"].reshape(BATCH, SEQ, C)
```

```python
from contextlib import ExitStack

import concourse.bass as bass
from concourse import mybir

F32 = mybir.dt.float32
F32R = mybir.dt.float32r
ACT = mybir.ActivationFunctionType
ALU = mybir.AluOpType
AX = mybir.AxisListType
ds = bass.ds

P = 128
BATCH, SEQ, C = 8, 512, 128
HEADS, DH = 16, 64
CHUNKS = HEADS
GT = SEQ // HEADS
NPOS = GT * CHUNKS
QUADS = BATCH * SEQ // P
GQ = P // GT
QB = SEQ // P
IT = NPOS // P
KQ = GQ * IT
SQ = QB
KN = SQ * KQ
GN = SQ * GQ
E_S, E_R, HID = 2, 8, 512
E = E_S + E_R
HT = HID // P
EPS_LN = 1e-5
EPS_RMS = float(2.0 ** -23)
NEG = -1.0
TOPK = 2
RING_S, RING_T, RING_P = 2, 2, 4
STEPS = QUADS // SQ
X_PIECES = 4
MOD_STEPS, MOD_AT = 21, 18
TAIL_DVE = ("y_gated", "x_new", "stats", "mean_var", "var_eps", "rstd_a", "rstd_b", "rstd", "z", "z_scaled", "u",
            "mean_square", "inv_rms_a", "inv_rms_b", "inv_rms", "un", "un_low")
TAIL_ACT = ("ln_var", "rstd_0", "squares", "ln_square", "inv_rms_0", "un_high", "uT")
GATE_DVE = ("one_plus", "score", "total", "higher", "same", "inv_total", "same_lower", "before", "rank", "chosen",
            "gate")
GATE_ACT = ("exp_logit",)
T_LAG = 3
QK_AT, V_AT = (0, 4, 8, 12), (2, 6, 9, 11)
Y_AT = (12, 13, 14, 15)
PV_LAG = 10
FN, PN = 4 * SQ, GN // 2
RING_H, RING_G, RING_Y, RING_W = 2, 4, 3, 4
W2_LAG, Y_LAG, SEL, BACK = 3, 4, 2, 8


class Count:

    def __init__(self, eng, n):
        self.eng, self.n = eng, n

    def __call__(self, sem, per, count):
        if isinstance(self.n, int):
            if self.n * per + count > 0:
                self.eng.wait_ge(sem, self.n * per + count)
        else:
            self.eng.wait_ge(sem, self.n * per + count)


def chain(eng, sem):
    seen = [0]

    def link(ins):
        seen[0] += 1
        ins.then_inc(sem, 1)
        eng.wait_ge(sem, seen[0])

    return link


def prepare(nc, t, dram):
    with ExitStack() as ctx:
        sem = lambda name: ctx.enter_context(nc.semaphore(name))
        sb = lambda name, shape, dt=F32: ctx.enter_context(nc.sbuf_tensor(name, shape, dt))
        loaded_c, loaded_w, small_loaded = map(sem, ("loaded_c", "loaded_w", "small_loaded"))
        loaded_x = [sem("loaded_x%d" % i) for i in range(X_PIECES)]
        ident_ready, exp_c, silu_ready, modT_done, modB_done = map(
            sem, ("ident_ready", "exp_c", "silu_ready", "modT_done", "modB_done"))
        modB_copied, var_ready, std_ready, z_ready, zT_done = map(
            sem, ("modB_copied", "var_ready", "std_ready", "z_ready", "zT_done"))
        dchain, pchain = sem("dve_chain_a"), sem("pool_chain_a")
        cT, sc, ec = sb("cT", [P, BATCH]), sb("sc", [P, BATCH]), sb("ec", [P, BATCH])
        scB = sb("scB", [P, BATCH, P])
        wmod = sb("wmod", [P, 6 * C])
        z = sb("z", [P, QB, C])
        pmod = ctx.enter_context(nc.psum_tensor("pmod", [P, 2, 512], F32))
        pT = ctx.enter_context(nc.psum_tensor("pT", [P, 512], F32))
        pm = ctx.enter_context(nc.psum_tensor("pm", [P, 2, BATCH], F32))
        block = ctx.enter_context(nc.Block())

        @block.sync
        def _(sp):
            sp.dma_start(cT[:], dram["cT"]).then_inc(loaded_c, 16)
            sp.dma_start(wmod[:], dram["wmod"]).then_inc(loaded_c, 16)
            for i, loaded in enumerate(loaded_x):
                piece = slice(i * QUADS // X_PIECES, (i + 1) * QUADS // X_PIECES)
                sp.dma_start(t["x"][:, piece, :], dram["x"].rearrange("(q p) c -> p q c", p=P)[:, piece, :]
                             ).then_inc(loaded, 16)
            for name in ("wq", "wk", "wv", "wo"):
                sp.dma_start(t[name][:], dram[name + "T"]).then_inc(loaded_w, 16)
            for name in ("cent", "g2", "b1", "b2T"):
                sp.dma_start(t[name][:], dram[name]).then_inc(small_loaded, 16)
            sp.wait_ge(small_loaded, 4 * 16)
            sp.wait_ge(loaded_w, 4 * 16)
            for loaded in loaded_x:
                sp.wait_ge(loaded, 16)

        @block.gpsimd
        def _(pool):
            link = chain(pool, pchain)
            link(pool.memset(t["ident"][:], 0.0))
            pool.affine_select(out=t["ident"][:], in_=t["ident"][:], compare_op=ALU.not_equal, fill=1.0,
                               base=0, pattern=[[-1, P]], channel_multiplier=1).then_inc(ident_ready, 1)
            link(pool.memset(t["hT"][:, QUADS:QUADS + 2, :], 0.0))
            link(pool.memset(t["gate"][:, QUADS:QUADS + QB, :], 0.0))
            link(pool.memset(t["lower"][:], 1.0))
            link(pool.affine_select(out=t["lower"][:], in_=t["lower"][:], compare_op=ALU.is_gt, fill=0.0, base=0,
                                    pattern=[[1, E_R], [-1, E_R]], channel_multiplier=0))

        @block.scalar
        def _(act):
            act.wait_ge(loaded_c, 32)
            act.activation(ec[:], cT[:], ACT.Exp, scale=NEG).then_inc(exp_c, 1)
            act.preload_act_table_set("sqrt_and_others")
            for b in range(BATCH):
                if b == BATCH - 2:
                    act.wait_ge(var_ready, 1)
                    act.activation(t["rstd"][:], t["var"][:], ACT.Sqrt).then_inc(std_ready, 1)
                act.wait_ge(modB_done, b + 1)
                act.activation(t["modB"][:, :, b, :], pmod[:, b % 2, :].rearrange("p (k c) -> p k c", c=C),
                               ACT.Copy).then_inc(modB_copied, 1)

        @block.tensor
        def _(pe):
            pe.wait_ge(silu_ready, 1)
            for k in range(2):
                mm = pe.matmul(pm[:, k, :], wmod[:, k * C:(k + 1) * C], sc[:], start=True, stop=True)
            mm.then_inc(modT_done, 1)
            pe.wait_ge(silu_ready, 2)
            for b in range(BATCH):
                if b >= 2:
                    pe.wait_ge(modB_copied, b - 1)
                pe.matmul(pmod[:, b % 2, :], scB[:, b, :], wmod[:, 2 * C:6 * C], start=True,
                          stop=True).then_inc(modB_done, 1)
            pe.wait_ge(ident_ready, 1)
            pe.wait_ge(z_ready, 1)
            for q in range(QB):
                mm = pe.transpose(pT[:, q * P:(q + 1) * P], z[:, q, :], t["ident"][:])
            mm.then_inc(zT_done, 1)

        @block.vector
        def _(dve):
            link = chain(dve, dchain)
            dve.wait_ge(exp_c, 1)
            link(dve.tensor_scalar(ec[:], ec[:], 1.0, None, ALU.add))
            link(dve.reciprocal(ec[:], ec[:]))
            dve.tensor_tensor(sc[:], ec[:], cT[:], ALU.mult).then_inc(silu_ready, 1)
            dve.wait_ge(silu_ready, 1)
            dve.tensor_copy(scB[:], sc[:].unsqueeze(2).to_broadcast([P, BATCH, P])).then_inc(silu_ready, 1)
            layernorm_stats(dve, link, t, loaded_x)
            dve.tensor_scalar(t["var"][:], t["var"][:], EPS_LN, None, ALU.add).then_inc(var_ready, 1)
            dve.wait_ge(modT_done, 1)
            link(dve.tensor_copy(t["saT"][:], pm[:, 0, :]))
            link(dve.tensor_scalar(t["caT"][:], pm[:, 1, :], 1.0, None, ALU.add))
            dve.wait_ge(std_ready, 1)
            link(dve.reciprocal(t["rstd"][:], t["rstd"][:]))
            for q in range(QB):
                ins = dve.tensor_scalar(z[:, q, :], t["x"][:, q, :], t["mean"][:, q:q + 1], t["rstd"][:, q:q + 1],
                                        ALU.subtract, ALU.mult)
            ins.then_inc(z_ready, 1)
            dve.wait_ge(zT_done, 1)
            dve.tensor_scalar(t["hT"][:, 0:QB, :].rearrange("p q c -> p (q c)"), pT[:], t["caT"][:, 0:1],
                              t["saT"][:, 0:1], ALU.mult, ALU.add)
            dve.wait_ge(loaded_w, 4 * 16)
            link(dve.tensor_scalar(t["wq"][:], t["wq"][:], float(DH) ** -0.5, None, ALU.mult))


def layernorm_stats(dve, link, t, loaded_x):
    st = t["stats"]
    for q in range(QUADS):
        if q % (QUADS // X_PIECES) == 0:
            dve.wait_ge(loaded_x[q * X_PIECES // QUADS], 16)
        ins = dve.bn_stats(st[:, q, :], t["x"][:, q, :])
    link(ins)
    me, m2e, mo, m2o = (st[:, :, k] for k in (1, 2, 4, 5))
    link(dve.tensor_tensor(t["mean"][:], me, mo, ALU.add))
    link(dve.tensor_tensor(t["var"][:], me, mo, ALU.subtract))
    link(dve.tensor_scalar(t["mean"][:], t["mean"][:], 0.5, None, ALU.mult))
    link(dve.scalar_tensor_tensor(out=t["var"][:], in0=t["var"][:], scalar=C / 4.0, in1=t["var"][:],
                                  op0=ALU.mult, op1=ALU.mult))
    link(dve.tensor_tensor(t["var"][:], t["var"][:], m2e, ALU.add))
    link(dve.tensor_tensor(t["var"][:], t["var"][:], m2o, ALU.add))
    link(dve.tensor_scalar(t["var"][:], t["var"][:], 1.0 / C, None, ALU.mult))


def attend(nc, t, dram):
    with ExitStack() as ctx:
        sem = lambda name: ctx.enter_context(nc.semaphore(name))
        sb = lambda name, shape, dt=F32: ctx.enter_context(nc.sbuf_tensor(name, shape, dt))
        psum = lambda name, n: ctx.enter_context(nc.psum_tensor(name, [P, n, 512], F32))
        hq_ready, y_done, x_out, ms_done, uT_done, logit_done = map(
            sem, ("hq_ready", "y_done", "x_out", "ms_done", "uT_done", "logit_done"))
        tail_dve, tail_act, tail_pool, gate_dve, gate_act = map(
            sem, ("tail_dve", "tail_act", "tail_pool", "gate_dve", "gate_act"))
        mod_step_done, dve_turn = sem("mod_step_done"), sem("dve_turn")
        z_ready, zT_done, hT_ready = sem("z_ready1"), sem("zT_done1"), sem("hT_ready")
        qk_done, part_hi, part_lo, k_copied = sem("qk_done"), sem("part_hi"), sem("part_lo"), sem("k_copied")
        v_done, v_ready = sem("v_done"), sem("v_ready")
        pv_done, o_dve, o_act = sem("pv_done"), sem("o_dve"), sem("o_act")
        s_done, max_done, exp_done, rden_done, p_scaled, t_done, t_out = map(
            sem, ("s_done", "max_done", "exp_done", "rden_done", "p_scaled", "t_done", "t_out"))
        pool_turn = sem("pool_turn")

        hq = sb("hq", [P, 2, P])
        Q = sb("Q", [P, 2, GQ, NPOS], F32R)
        KH = sb("KH", [P, 2, GQ, NPOS], F32R)
        KL = sb("KL", [P, 2, GQ, NPOS], F32R)
        V = sb("V", [P, 2, GQ, IT, DH])
        prob = sb("prob", [P, RING_P, NPOS])
        PT = sb("PT", [P, GQ, IT, NPOS])
        O = sb("O", [P, CHUNKS // 2, P])
        nmax, den, rden = (sb(name, [P, RING_P]) for name in ("nmax", "den", "rden"))
        xq, uq, unq, uT, gu, sq = (sb(name, [P, C]) for name in ("xq", "uq", "unq", "uT", "gu", "sq"))
        stats, meanvar = sb("bstats", [P, 6]), sb("meanvar", [P, 2])
        ve, ms = sb("ve", [P, 2]), sb("ms", [P, 2])
        rstd2, rr, step, total = (sb(name, [P, 1]) for name in ("rstd2", "rr", "step", "total"))
        score, rank = sb("score", [P, E_R]), sb("rank", [P, E_R])
        higher, same = sb("higher", [P, E_R, E_R]), sb("same", [P, E_R, E_R])
        ps_s, ps_t, ps_o, ps_qk, ps_vy = (
            psum("ps_s", RING_S), psum("ps_t", RING_T), psum("ps_o", 2), psum("ps_qk", 1), psum("ps_vy", 1))
        ps_v, ps_y = ps_vy[:, 0, 0:IT * DH], ps_vy[:, 0, IT * DH:IT * DH + C]
        hT, ident = t["hT"], t["ident"]
        HALF = (slice(0, DH), slice(DH, P))

        def within(n, per, index):
            return not isinstance(n, int) or 0 <= n * per + index < STEPS * per

        def tail(cnt, qt, name):
            for done, names in ((tail_dve, TAIL_DVE), (tail_act, TAIL_ACT), (gate_dve, GATE_DVE), (gate_act, GATE_ACT)):
                if name in names:
                    cnt(done, len(names) * SQ, len(names) * qt + names.index(name) + 1)

        def tail_at(n, k, offset):
            qt = (k - offset) // KQ - 2
            return qt if (k - offset) % KQ == 0 and within(n, SQ, qt) else None

        def fill_of(k):
            return 4 * (k // KQ + 1) + QK_AT.index(k % KQ)

        FIRST = -1

        def qk_bank(n, f):
            return (ps_qk[:, 0], ps_s[:, 0], ps_s[:, 1], ps_t[:, 0])[f] if n is FIRST else ps_qk[:, 0]

        def v_bank(n, slot):
            return ((ps_v, ps_t[:, 1, 0:IT * DH], ps_o[:, 0, 0:IT * DH], ps_o[:, 1, 0:IT * DH])[slot] if n is FIRST
                    else ps_v)

        def project(pe, n, k):
            cnt, quad, kq = Count(pe, n), k // KQ, k % KQ
            nxt = (quad + 1) % 2
            if kq in QK_AT:
                f = QK_AT.index(kq)
                w, half = (t["wk"], t["wq"])[f % 2], f // 2
                bank = qk_bank(n, f)
                if n is not FIRST:
                    cnt(part_lo, FN * 2, 2 * fill_of(k))
                if f == 0:
                    cnt(hq_ready, SQ, quad + 2)
                for c in range(4):
                    pair = 4 * half + c
                    mm = pe.matmul(bank[:, c * P:(c + 1) * P], w[:, pair * P:(pair + 1) * P], hq[:, nxt, :],
                                   start=True, stop=True)
                mm.then_inc(qk_done, 1)
            if kq in V_AT:
                slot = V_AT.index(kq)
                bank = v_bank(n, slot)
                if n is not FIRST:
                    cnt(v_ready, GN, GQ * (quad + 1) + slot)
                    tail(cnt, quad - 2, "y_gated")
                wv = t["wv"][:].rearrange("p (a c d) -> p c a d", c=4, d=DH)
                for c in range(4):
                    mm = pe.matmul(bank[c * GT:(c + 1) * GT, :],
                                   hq[:, nxt, slot * GT:(slot + 1) * GT], wv[:, c], start=True, stop=True,
                                   tile_position=(0, c * GT))
                mm.then_inc(v_done, 1)

        def pe_tile(pe, n, k):
            cnt, kq = Count(pe, n), k % KQ
            if within(n, KN, k):
                par, slot, i = (k // KQ) % 2, kq // IT, k % IT
                if kq == 0:
                    cnt(part_lo, FN * 2, 8 * (k // KQ + 1))
                    cnt(v_ready, GN, GQ * (k // KQ + 1))
                    cnt(k_copied, 64 * SQ, 64 * (k // KQ + 1))
                cnt(exp_done, KN, k - RING_S + 1)
                for part in (KH, KL):
                    mm = pe.matmul(ps_s[:, k % RING_S, :], Q[:, par, slot, i * P:(i + 1) * P],
                                   part[:, par, slot, :], start=(part is KH), stop=(part is KL))
                mm.then_inc(s_done, 1)
                project(pe, n, k)
            kt = k - T_LAG
            if within(n, KN, kt):
                cnt(p_scaled, KN, kt + 1)
                cnt(t_out, KN, kt - RING_T + 1)
                for a in range(IT):
                    mm = pe.transpose(ps_t[:, kt % RING_T, a * P:(a + 1) * P],
                                      prob[:, kt % RING_P, a * P:(a + 1) * P], ident[:])
                mm.then_inc(t_done, 1)
            p = (k - PV_LAG) // 8
            parts = ((k - PV_LAG) % 8 // 2 * 2 + i for i in range(2)) if (k - PV_LAG) % 2 else ()
            for j in parts if within(n, PN, p) else ():
                half, a = j // IT, j % IT
                cols = slice(half * 256, half * 256 + 256)
                if a == 0:
                    cnt(t_out, KN, 8 * p + IT + 2 * (half + 1))
                if j == 0:
                    if isinstance(n, int) and n == 0 and p == 1:
                        pe.wait_ge(hT_ready, BATCH - 1)
                    if p % 2:
                        tail(cnt, k // KQ - 3, "exp_logit")
                    cnt(o_dve, 2 * PN, 2 * (p - 1))
                    cnt(o_act, 2 * PN, 2 * (p - 1))
                for m in range(2):
                    g = 2 * p + m
                    mm = pe.matmul(ps_o[HALF[m], p % 2, cols], V[:, (g // GQ) % 2, g % GQ, a, :],
                                   PT[:, g % GQ, a, cols], start=(j == 0), stop=(a == IT - 1),
                                   tile_position=(0, m * DH), skip_group_check=True)
                if j == 7:
                    mm.then_inc(pv_done, 1)
            qt = k // KQ - 1
            if kq in Y_AT and within(n, SQ, qt):
                if kq == Y_AT[0]:
                    cnt(o_dve, 2 * PN, 4 * (qt + 1))
                    cnt(o_act, 2 * PN, 4 * (qt + 1))
                    cnt(v_ready, GN, GQ * (qt + (3 if within(n, KN, k) else 2)))
                y_part = Y_AT.index(kq)
                for c in range(2 * y_part, 2 * y_part + 2):
                    mm = pe.matmul(ps_y, O[:, c, :], t["wo"][:, c * C:(c + 1) * C], start=(c == 0),
                                   stop=(c == CHUNKS // 2 - 1), skip_group_check=True)
                if y_part == len(Y_AT) - 1:
                    mm.then_inc(y_done, 1)
            pe_early(pe, n, k)
            qt = tail_at(n, k, 13)
            if qt is not None:
                p = 2 * (k // KQ - 1) + 1
                count = 2 * (p + 1) if within(n, PN, p) else 2 * (p - 1)
                cnt(o_dve, 2 * PN, count)
                cnt(o_act, 2 * PN, count)
                tail(cnt, qt, "un")
                pe.transpose(ps_o[:, 1, 0:P], uq[:], ident[:])
                pe.transpose(ps_o[:, 1, P:2 * P], unq[:], ident[:]).then_inc(uT_done, 1)
            qt = tail_at(n, k, 16)
            if qt is not None:
                tail(cnt, qt, "un_low")
                pe.matmul(ps_o[:, 1, 2 * P:2 * P + E_R], uT[:], t["cent"][:], start=True,
                          stop=True).then_inc(logit_done, 1)

        def by_group(rows, bank):
            return bank[rows, :].rearrange("p (c g t) -> p c g t", c=4, g=GQ)

        def into_groups(buf, rows, par, half, odd):
            v = buf[rows, par, :, :].rearrange("p g (c o t) -> p o c g t", o=2, t=GT)
            return v[:, odd, 4 * half:4 * half + 4]

        def o_half(m, p, odd):
            slot = (2 * p + m) % GQ
            return (O[HALF[odd], :, slot * GT:(slot + 1) * GT],
                    ps_o[HALF[m], p % 2, :].rearrange("p (c o t) -> p o c t", o=2, t=GT)[:, odd])

        def before_o(cnt, p, odd):
            if odd == 0:
                cnt(pv_done, PN, p + 1)
                if p % 2 == 0:
                    cnt(y_done, SQ, p // 2)

        def act_project(act, n, k):
            cnt = Count(act, n)
            for odd in range(2):
                if (k - odd) % KQ in QK_AT:
                    ks = k - odd
                    f = QK_AT.index(ks % KQ)
                    cnt(qk_done, FN, fill_of(ks) + 1)
                    act.activation(into_groups((KH, Q)[f % 2], HALF[0], (ks // KQ + 1) % 2, f // 2, odd),
                                   by_group(HALF[odd], qk_bank(n, f)), ACT.Copy).then_inc(part_hi, 1)

        def act_tile(act, n, k):
            cnt = Count(act, n)
            if within(n, KN, k):
                cnt(max_done, KN, k + 1)
                cnt(t_done, KN, k - RING_P + 1)
                r = k % RING_P
                act.activation(prob[:, r, :], ps_s[:, k % RING_S, :], ACT.Exp, bias=nmax[:, r:r + 1],
                               accum_out=den[:, r:r + 1]).then_inc(exp_done, 1)
                act_project(act, n, k)
            kt = k - T_LAG
            if within(n, KN, kt):
                gt, it = kt // IT, kt % IT
                cnt(t_done, KN, kt + 1)
                if it == 0:
                    cnt(pv_done, PN, gt // 2 - 1)
                act.activation(PT[:, gt % GQ, :, it * P:(it + 1) * P],
                               ps_t[:, kt % RING_T, :].rearrange("p (a q) -> p a q", a=IT),
                               ACT.Copy).then_inc(t_out, 1)
            p, odd = (k - PV_LAG) // 8 - 1, (k - PV_LAG) % 8
            if odd < 2 and within(n, PN, p):
                before_o(cnt, p, odd)
                o, sums = o_half(1, p, odd)
                act.activation(o, sums, ACT.Copy).then_inc(o_act, 1)
            act_tail(act, n, k)

        def act_tail(act, n, k):
            cnt = Count(act, n)
            qt = tail_at(n, k, 2)
            if qt is not None:
                tail(cnt, qt, "var_eps")
                act.activation(ve[:, 1:2], ve[:, 0:1], ACT.Ln).then_inc(tail_act, 1)
                tail(cnt, qt, "ln_var")
                act.activation(ve[:, 1:2], ve[:, 1:2], ACT.Exp, scale=-0.5).then_inc(tail_act, 1)
            qt = tail_at(n, k, 8)
            if qt is not None:
                tail(cnt, qt, "u")
                act.activation(sq[:], uq[:], ACT.Square, accum_out=ms[:, 0:1]).then_inc(tail_act, 1)
            qt = tail_at(n, k, 10)
            if qt is not None:
                tail(cnt, qt, "mean_square")
                act.activation(ms[:, 1:2], ms[:, 0:1], ACT.Ln).then_inc(tail_act, 1)
                tail(cnt, qt, "ln_square")
                act.activation(ms[:, 1:2], ms[:, 1:2], ACT.Exp, scale=-0.5).then_inc(tail_act, 1)
            qt = tail_at(n, k, 14)
            if qt is not None:
                cnt(uT_done, SQ, qt + 1)
                act.activation(t["unH"][:, ds((n * SQ + qt) * P, P)], ps_o[:, 1, P:2 * P], ACT.Copy
                               ).then_inc(tail_act, 1)
                cnt(logit_done, SQ, qt)
                act.activation(uT[:], ps_o[:, 1, 0:P], ACT.Copy).then_inc(tail_act, 1)
            qt = tail_at(n, k, 17)
            if qt is not None:
                cnt(logit_done, SQ, qt + 1)
                tail(cnt, qt - 1, "gate")
                act.activation(score[:], ps_o[:, 1, 2 * P:2 * P + E_R], ACT.Exp, scale=NEG).then_inc(gate_act, 1)

        def dve_tail(dve, n, k):
            cnt = Count(dve, n)
            flat = "p q c -> p (q c)"
            mod = lambda m: t["modB"][:, m, ds(n + qt // SQ, 1), :].rearrange(flat)
            this = score[:].unsqueeze(2).to_broadcast([P, E_R, E_R])
            other = score[:].unsqueeze(1).to_broadcast([P, E_R, E_R])
            qt = tail_at(n, k, 0)
            if qt is not None:
                cnt(y_done, SQ, qt + 1)
                cnt(x_out, SQ, qt)
                dve.tensor_tensor(xq[:], ps_y, mod(0), ALU.mult).then_inc(tail_dve, 1)
                tail(cnt, qt, "y_gated")
                dve.tensor_tensor(xq[:], xq[:], t["x"][:, ds(n * SQ + qt, 1), :].rearrange(flat), ALU.add).then_inc(tail_dve, 1)
            qt = tail_at(n, k, 1)
            if qt is not None:
                tail(cnt, qt, "x_new")
                dve.bn_stats(stats[:], xq[:]).then_inc(tail_dve, 1)
                tail(cnt, qt, "stats")
                dve.sem_inc(dve_turn, 1)
                dve.bn_aggr(meanvar[:], stats[:]).then_inc(tail_dve, 1)
                tail(cnt, qt, "mean_var")
                dve.tensor_scalar(ve[:, 0:1], meanvar[:, 1:2], EPS_LN, None, ALU.add).then_inc(tail_dve, 1)
            qt = tail_at(n, k, 4)
            if qt is not None:
                tail(cnt, qt, "rstd_0")
                dve.tensor_scalar(step[:], ve[:, 1:2], ve[:, 1:2], ve[:, 0:1], ALU.mult, ALU.mult
                                  ).then_inc(tail_dve, 1)
                tail(cnt, qt, "rstd_a")
                dve.tensor_scalar(step[:], step[:], -0.5, 1.5, ALU.mult, ALU.add).then_inc(tail_dve, 1)
                tail(cnt, qt, "rstd_b")
                dve.tensor_scalar(rstd2[:], step[:], ve[:, 1:2], None, ALU.mult).then_inc(tail_dve, 1)
                tail(cnt, qt, "rstd")
                cnt(uT_done, SQ, qt)
                dve.tensor_scalar(uq[:], xq[:], meanvar[:, 0:1], rstd2[:], ALU.subtract, ALU.mult
                                  ).then_inc(tail_dve, 1)
            qt = tail_at(n, k, 7)
            if qt is not None:
                tail(cnt, qt, "z")
                dve.tensor_tensor(uq[:], uq[:], mod(2), ALU.mult).then_inc(tail_dve, 1)
                tail(cnt, qt, "z_scaled")
                dve.tensor_tensor(uq[:], uq[:], mod(1), ALU.add).then_inc(tail_dve, 1)
            qt = tail_at(n, k, 9)
            if qt is not None:
                tail(cnt, qt, "squares")
                dve.tensor_scalar(ms[:, 0:1], ms[:, 0:1], 1.0 / C, EPS_RMS, ALU.mult, ALU.add).then_inc(tail_dve, 1)
            qt = tail_at(n, k, 12)
            if qt is not None:
                tail(cnt, qt, "inv_rms_0")
                dve.tensor_scalar(step[:], ms[:, 1:2], ms[:, 1:2], ms[:, 0:1], ALU.mult, ALU.mult
                                  ).then_inc(tail_dve, 1)
                tail(cnt, qt, "inv_rms_a")
                dve.tensor_scalar(step[:], step[:], -0.5, 1.5, ALU.mult, ALU.add).then_inc(tail_dve, 1)
                tail(cnt, qt, "inv_rms_b")
                dve.tensor_scalar(rr[:], step[:], ms[:, 1:2], None, ALU.mult).then_inc(tail_dve, 1)
                tail(cnt, qt, "inv_rms")
                dve.tensor_scalar(unq[:], uq[:], rr[:], None, ALU.mult).then_inc(tail_dve, 1)
            qt = tail_at(n, k, 15)
            if qt is not None:
                tail(cnt, qt, "uT")
                cols = ds((n * SQ + qt) * P, P)
                dve.tensor_tensor(t["unL"][:, cols], ps_o[:, 1, P:2 * P], t["unH"][:, cols], ALU.subtract
                                  ).then_inc(tail_dve, 1)
            qt = tail_at(n, k, 18)
            if qt is not None:
                tail(cnt, qt, "exp_logit")
                dve.tensor_scalar(score[:], score[:], 1.0, None, ALU.add).then_inc(gate_dve, 1)
                tail(cnt, qt, "one_plus")
                dve.reciprocal(score[:], score[:]).then_inc(gate_dve, 1)
            qt = tail_at(n, k, 19)
            if qt is not None:
                tail(cnt, qt, "score")
                dve.tensor_reduce(total[:], score[:], AX.X, ALU.add).then_inc(gate_dve, 1)
                dve.tensor_tensor(higher[:], other, this, ALU.is_gt).then_inc(gate_dve, 1)
                dve.tensor_tensor(same[:], other, this, ALU.is_equal).then_inc(gate_dve, 1)
            qt = tail_at(n, k, 20)
            if qt is not None:
                tail(cnt, qt, "same")
                dve.reciprocal(total[:], total[:]).then_inc(gate_dve, 1)
                dve.tensor_tensor(same[:], same[:], t["lower"][:], ALU.mult).then_inc(gate_dve, 1)
                tail(cnt, qt, "same_lower")
                dve.tensor_tensor(higher[:], higher[:], same[:], ALU.add).then_inc(gate_dve, 1)
            qt = tail_at(n, k, 23)
            if qt is not None:
                tail(cnt, qt, "before")
                dve.tensor_reduce(rank[:], higher[:], AX.X, ALU.add).then_inc(gate_dve, 1)
                tail(cnt, qt, "rank")
                dve.scalar_tensor_tensor(out=rank[:], in0=rank[:], scalar=TOPK - 0.5, in1=score[:], op0=ALU.is_lt,
                                         op1=ALU.mult).then_inc(gate_dve, 1)
            qt = tail_at(n, k, 24)
            if qt is not None:
                tail(cnt, qt, "chosen")
                dve.tensor_scalar(t["gate"][:, ds(n * SQ + qt, 1), :].rearrange(flat), rank[:], total[:], None, ALU.mult
                                  ).then_inc(gate_dve, 1)

        def mod_step(dve, i):
            if i == MOD_STEPS - 1:
                dve.tensor_scalar(t["modB"][:, 2, :, :], t["modB"][:, 2, :, :], 1.0, None, ALU.add
                                  ).then_inc(mod_step_done, 1)
                return
            half = slice(i // 10 * BATCH // 2, (i // 10 + 1) * BATCH // 2)
            g, sign = t["modB"][:, (0, 3)[i // 5 % 2], half, :], hT[:, 0:BATCH // 2, :]
            if i:
                dve.wait_ge(mod_step_done, i)
            if i % 5 == 0:
                dve.tensor_scalar(sign, g, 0.0, 2.0, ALU.is_ge, ALU.mult).then_inc(mod_step_done, 1)
            if i % 5 == 1:
                dve.tensor_scalar(sign, sign, -1.0, None, ALU.add).then_inc(mod_step_done, 1)
            if i % 5 == 3:
                dve.tensor_scalar(g, g, 0.25, None, ALU.max).then_inc(mod_step_done, 1)
            if i % 5 in (2, 4):
                dve.tensor_tensor(g, g, sign, ALU.mult).then_inc(mod_step_done, 1)

        def dve_early(dve, n, k):
            if not (isinstance(n, int) and n == 0):
                return
            if k % 2 == 0 and 1 <= k // 2 < BATCH:
                b = k // 2
                if b > 2:
                    dve.wait_ge(zT_done, b - 2)
                for q in range(QB):
                    kq = b * QB + q
                    ins = dve.tensor_scalar(O[:, b % 2 * QB + q, :], t["x"][:, kq, :], t["mean"][:, kq:kq + 1],
                                            t["rstd"][:, kq:kq + 1], ALU.subtract, ALU.mult)
                ins.then_inc(z_ready, 1)
            if k % 2 and 1 <= k // 2 - 1 < BATCH:
                b = k // 2 - 1
                dve.wait_ge(zT_done, b)
                dve.tensor_scalar(hT[:, b * QB:(b + 1) * QB, :].rearrange("p q c -> p (q c)"), ps_o[:, 1, :],
                                  t["caT"][:, b:b + 1], t["saT"][:, b:b + 1], ALU.mult, ALU.add).then_inc(hT_ready, 1)
            if k == MOD_AT:
                dve.wait_ge(hq_ready, QB)
            for i in range(2 * (k - MOD_AT), 2 * (k - MOD_AT) + 2):
                if 0 <= i < MOD_STEPS:
                    mod_step(dve, i)
            if k == 2 * KQ - 1:
                dve.wait_ge(mod_step_done, MOD_STEPS)

        def pe_early(pe, n, k):
            if isinstance(n, int) and n == 0 and k % 2 == 0 and 1 <= k // 2 - 1 < BATCH:
                b = k // 2 - 1
                pe.wait_ge(z_ready, b)
                if b > 1:
                    pe.wait_ge(hT_ready, b - 1)
                for q in range(QB):
                    mm = pe.transpose(ps_o[:, 1, q * P:(q + 1) * P], O[:, b % 2 * QB + q, :], ident[:])
                mm.then_inc(zT_done, 1)

        def dve_project(dve, n, k):
            cnt, quad, kq = Count(dve, n), k // KQ, k % KQ
            for late in (1, 2):
                if (k - late) % KQ in QK_AT:
                    ks, odd = k - late, late - 1
                    f = QK_AT.index(ks % KQ)
                    par, half = (ks // KQ + 1) % 2, f // 2
                    cnt(part_hi, 2 * FN, 2 * fill_of(ks) + odd + 1)
                    hi, lo = ((KH, KL), (Q, Q))[f % 2]
                    dve.tensor_tensor(into_groups(lo, HALF[f % 2], par, half, odd), by_group(HALF[odd], qk_bank(n, f)),
                                      into_groups(hi, HALF[0], par, half, odd), ALU.subtract).then_inc(part_lo, 1)
            if kq in V_AT:
                slot = V_AT.index(kq)
                cnt(v_done, GN, GQ * (quad + 1) + slot + 1)
                cnt(pv_done, PN, 2 * (quad - 1) + slot // 2 + 1)
                dve.tensor_copy(V[:, (quad + 1) % 2, slot, :, :], v_bank(n, slot).rearrange("p (a d) -> p a d", d=DH)
                                ).then_inc(v_ready, 1)

        def dve_tile(dve, n, k):
            cnt = Count(dve, n)
            kr, r = k - 1, (k - 1) % RING_P
            if within(n, KN, kr):
                cnt(exp_done, KN, kr + 1)
                dve.reciprocal(rden[:, r:r + 1], den[:, r:r + 1]).then_inc(rden_done, 1)
            r = k % RING_P
            if within(n, KN, k):
                cnt(s_done, KN, k + 1)
                dve.tensor_reduce(nmax[:, r:r + 1], ps_s[:, k % RING_S, :], AX.X, ALU.max,
                                  negate=True).then_inc(max_done, 1)
            p, odd = (k - PV_LAG) // 8 - 1, (k - PV_LAG) % 8
            if odd < 2 and within(n, PN, p):
                before_o(cnt, p, odd)
                o, sums = o_half(0, p, odd)
                dve.tensor_copy(o, sums).then_inc(o_dve, 1)
            if within(n, KN, k):
                dve_project(dve, n, k)
            dve_tail(dve, n, k)
            dve_early(dve, n, k)

        def pool_tail(pool, n, k):
            cnt, qt = Count(pool, n), k // KQ - 2
            if k % KQ == 8 and within(n, SQ, qt):
                if isinstance(n, int) and n == 0 and qt == 0:
                    pool.wait_ge(mod_step_done, MOD_STEPS)
                tail(cnt, qt, "u")
                gb = t["modB"][:, 3, ds(n + qt // SQ, 1), :].rearrange("p q c -> p (q c)")
                pool.sem_inc(pool_turn, 1)
                pool.tensor_tensor(gu[:], uq[:], gb, ALU.mult).then_inc(tail_pool, 1)
                cnt(tail_pool, SQ, qt + 1)
                pool.sem_inc(pool_turn, 1)
                pool.tensor_tensor(t["x"][:, ds(n * SQ + qt, 1), :].rearrange("p q c -> p (q c)"), xq[:], gu[:],
                                   ALU.add).then_inc(x_out, 1)

        def pool_tile(pool, n, k):
            if within(n, KN, k):
                pool_scale(pool, n, k)
            pool_tail(pool, n, k)

        def pool_scale(pool, n, k):
            cnt, r = Count(pool, n), k % RING_P
            cnt(rden_done, KN, k + 1)
            pool.sem_inc(pool_turn, 1)
            pool.tensor_scalar(prob[:, r, :], prob[:, r, :], rden[:, r:r + 1], 1.0, ALU.mult,
                               ALU.mult).then_inc(p_scaled, 1)
            if k % KQ == 1:
                quad = k // KQ
                cnt(qk_done, FN, 4 * (quad + 1))
                if isinstance(n, int) and n == 0 and quad == 2:
                    pool.wait_ge(hT_ready, BATCH - 1)
                pool.tensor_copy(hq[:, quad % 2, :], hT[:, ds(n * SQ + quad + 2, 1), :].rearrange("p q c -> p (q c)")
                                 ).then_inc(hq_ready, 1)

        def copy_keys(sp, n, quad):
            cnt, nxt = Count(sp, n), (quad + 1) % 2
            for half in range(2):
                for buf, ready in ((KH, part_hi), (KL, part_lo)):
                    cnt(ready, 2 * FN, 2 * (4 * (quad + 1) + 2 * half + 1))
                    cols = slice(8 * half * GT, 8 * (half + 1) * GT)
                    sp.dma_start(buf[HALF[1], nxt, :, cols].bitcast(F32),
                                 buf[HALF[0], nxt, :, cols].bitcast(F32)).then_inc(k_copied, 16)

        def steps(eng, tile):
            for k in range(KN):
                tile(eng, 0, k)
            with eng.Fori(1, STEPS) as n:
                for k in range(KN):
                    tile(eng, n, k)

        block = ctx.enter_context(nc.Block())

        @block.sync
        def _(sp):
            copy_keys(sp, FIRST, SQ - 1)
            with sp.Fori(0, STEPS) as n:
                for quad in range(SQ):
                    copy_keys(sp, n, quad)
            sp.wait_ge(k_copied, 64 * (QUADS + 1))
            sp.wait_ge(hq_ready, QUADS + 2)
            for e in range(RING_W):
                load_expert(sp, t, dram, e)

        @block.tensor
        def _(pe):
            for k in range(KN - KQ, KN):
                project(pe, FIRST, k)
            steps(pe, pe_tile)
            for k in range(2 * KQ + 9):
                pe_tile(pe, STEPS, k)

        @block.scalar
        def _(act):
            act.preload_act_table_set("natural_log_exp_and_others")
            for k in range(KN - KQ, KN):
                act_project(act, FIRST, k)
            steps(act, act_tile)
            for k in range(2 * KQ + 9):
                act_tile(act, STEPS, k)

        @block.vector
        def _(dve):
            for k in range(KN - KQ, KN):
                dve_project(dve, FIRST, k)
            steps(dve, dve_tile)
            for k in range(2 * KQ + 9):
                dve_tile(dve, STEPS, k)

        @block.gpsimd
        def _(pool):
            for quad in range(2):
                pool.tensor_copy(hq[:, quad, :], hT[:, quad, :]).then_inc(hq_ready, 1)
            steps(pool, pool_tile)
            for k in range(2 * KQ + 9):
                pool_tile(pool, STEPS, k)


def load_expert(sp, t, dram, e):
    w1, w2, i = (dram["w1s"], dram["w2s"], e) if e < E_S else (dram["w1r"], dram["w2r"], e - E_S)
    raw = t["hT"][:].rearrange("p q c -> p (q c)")[:, 2 * (e % RING_W) * HID:2 * (e % RING_W + 1) * HID]
    sp.dma_start(raw[:, 0:HID], w1[i]).then_inc(t["w_loaded"][e % RING_W], 16)
    sp.dma_start(raw[:, HID:].rearrange("p (h c) -> p h c", h=HT), w2[i].rearrange("(h p) c -> p h c", p=P)
                 ).then_inc(t["w_loaded"][e % RING_W], 16)


def mix(nc, t, dram):
    with ExitStack() as ctx:
        sem = lambda name: ctx.enter_context(nc.semaphore(name))
        sb = lambda name, shape, dt=F32: ctx.enter_context(nc.sbuf_tensor(name, shape, dt))
        h_done, g_ready, g_hi, g_lo, w2_done = map(sem, ("h_done", "g_ready", "g_hi", "g_lo", "w2_done"))
        y_gated, acc_done, gate_done, gate_out = sem("y_gated"), sem("acc_done"), sem("gate_done"), sem("gate_out")
        gq_ready, gT_done, gT_hi, gT_lo, back_done, res_ready, stored = map(
            sem, ("gq_ready", "gT_done", "gT_hi", "gT_lo", "back_done", "res_ready", "stored"))
        w_scaled, w_hi, w_lo, sel_ready = sem("w_scaled"), sem("w_hi"), sem("w_lo"), sem("sel_ready")

        GH, GL = sb("GH", [P, RING_G, 512], F32R), sb("GL", [P, RING_G, 512], F32R)
        res = sb("res", [P, QB, C])
        gq = sb("gq", [P, QB, E_R])
        gT = sb("gT", [P, 512], F32R)
        sel = sb("sel", [P, E_R, P], F32R)
        LOW = 32
        G = sb("G", [P, RING_G, 512])
        acc, part = sb("acc", [P, 512])[:], sb("part", [P, 3, 512])
        psum = lambda name, n: ctx.enter_context(nc.psum_tensor(name, [P, n, 512], F32))
        p_h, p_y, p_g, p_t = psum("p_h", RING_H), psum("p_y", RING_Y), psum("p_g", 2), psum("p_t", 1)
        raw = t["hT"][:].rearrange("p q c -> p (q c)")

        units = [(e, h) for e in range(E) for h in range(HT)]
        U = len(units)
        SUMS = 1 + E_R
        sum_of = lambda e: max(0, e - E_S + 1)
        end_of = lambda s: (E_S + s) * HT - 1

        def within(n, per, index):
            return not isinstance(n, int) or 0 <= n * per + index < BATCH * per

        def raw_of(e):
            w = raw[:, 2 * (e % RING_W) * HID:2 * (e % RING_W + 1) * HID]
            return w[:, 0:HID], w[:, HID:]

        def sum_at(u, lag):
            v = u - lag
            for s in range(SUMS):
                for back in (0, 1):
                    if end_of(s) - back * U == v:
                        return s - back * SUMS
            return None

        def pe_unit(pe, n, u):
            cnt = Count(pe, n)
            if within(n, U, u):
                e, h = units[u]
                if isinstance(n, int) and n == 0 and h == 0:
                    pe.wait_ge(w_lo, 2 * e + 1)
                cnt(g_ready, U, u - RING_H + 1)
                w = slice(h * P, (h + 1) * P)
                for w1, un in (("w1H", "unH"), ("w1H", "unL"), ("w1L", "unH")):
                    mm = pe.matmul(p_h[:, u % RING_H, :], t[w1][:, e, w], t[un][:, ds(n * 512, 512)],
                                   start=(w1 == "w1H" and un == "unH"), stop=(w1 == "w1L"))
                mm.then_inc(h_done, 1)
                if u == 1:
                    cnt(gq_ready, 1, 1)
                    cnt(res_ready, 2, -2)
                    for q in range(QB):
                        mm = pe.transpose(p_t[0:E_R, 0, q * P:(q + 1) * P], gq[:, q, :], t["ident"][:])
                    mm.then_inc(gT_done, 1)
                s = sum_of(e)
                if s and u == end_of(s) - SEL:
                    if s == 1:
                        cnt(gT_lo, 1, 1)
                        if isinstance(n, int) and n == 0:
                            pe.wait_ge(sel_ready, 2)
                    cnt(gate_out, E_R, s - 2)
                    pe.matmul(p_g[:, s % 2, :], sel[:, s - 1, :], gT[:], start=True, stop=True).then_inc(gate_done, 1)
            v = u - W2_LAG
            if within(n, U, v):
                e, h = units[v % U]
                s = sum_of(e)
                first = (e, h) == (0, 0) or (s and h == 0)
                closes = v % U == end_of(s)
                if first:
                    cnt(y_gated, SUMS, s - RING_Y + 1 if v >= 0 else s - SUMS - RING_Y + 1)
                if isinstance(n, int) and n == 0 and h == 0:
                    pe.wait_ge(w_lo, 2 * e + 2)
                cnt(g_lo, U, v + 1)
                for i, (w2, g) in enumerate((("w2H", GH), ("w2H", GL), ("w2L", GH))):
                    mm = pe.matmul(p_y[:, s % RING_Y, :], t[w2][:, e, h * P:(h + 1) * P], g[:, v % RING_G, :],
                                   start=bool(first and i == 0), stop=bool(closes and i == 2))
                mm.then_inc(w2_done, 1)
            if u == BACK and within(n, 1, -1):
                cnt(acc_done, E_R, 0)
                cnt(gT_lo, 1, 1 if within(n, U, u) else 0)
                for q in range(QB):
                    mm = pe.transpose(p_t[:, 0, q * P:(q + 1) * P], acc[:, q * P:(q + 1) * P], t["ident"][:])
                mm.then_inc(back_done, 1)

        W_AT = (0, 2)

        def act_weights(act, e, k):
            if k == 0:
                act.wait_ge(w_scaled, e + 1)
            else:
                act.wait_ge(t["w_loaded"][e % RING_W], 32 * (e // RING_W + 1))
            act.activation(t[("w1H", "w2H")[k]][:, e, :], raw_of(e)[k], ACT.Copy).then_inc(w_hi, 1)

        def act_unit(act, n, u):
            cnt = Count(act, n)
            if within(n, U, u):
                cnt(h_done, U, u + 1)
                cnt(g_lo, U, u - RING_G + 1)
                act.activation(G[:, u % RING_G, :], p_h[:, u % RING_H, :], ACT.Gelu,
                               bias=t["b1"][:, u:u + 1]).then_inc(g_ready, 1)
            v = u - 1
            if within(n, U, v):
                cnt(w2_done, U, v - RING_G + 1)
                cnt(g_ready, U, v + 1)
                act.activation(GH[:, v % RING_G, :], G[:, v % RING_G, :], ACT.Copy).then_inc(g_hi, 1)
            if within(n, U, u):
                if u == 2:
                    cnt(gT_done, 1, 1)
                    cnt(gate_done, E_R, 0)
                    if isinstance(n, int) and n == 0:
                        act.wait_ge(sel_ready, 1)
                    act.activation(gT[0:E_R, :], p_t[0:E_R, 0, :], ACT.Copy).then_inc(gT_hi, 1)

        def dve_weights(dve, e, k):
            hi, lo = (("w1H", "w1L"), ("w2H", "w2L"))[k]
            dve.wait_ge(w_hi, 2 * e + k + 1)
            dve.tensor_tensor(t[lo][:, e, :], raw_of(e)[k], t[hi][:, e, :], ALU.subtract).then_inc(w_lo, 1)

        def part_free(cnt, si):
            before = si - 3
            block, s = before // SUMS, before % SUMS
            cnt(acc_done, E_R, block * E_R + max(s, 1))

        def dve_unit(dve, n, u):
            cnt, v = Count(dve, n), u - 1
            if within(n, U, v):
                cnt(g_hi, U, v + 1)
                dve.tensor_tensor(GL[:, v % RING_G, :], G[:, v % RING_G, :], GH[:, v % RING_G, :],
                                  ALU.subtract).then_inc(g_lo, 1)
            if within(n, U, u):
                if u == 3:
                    cnt(gT_hi, 1, 1)
                    dve.tensor_tensor(gT[LOW:LOW + E_R, :], p_t[0:E_R, 0, :], gT[0:E_R, :],
                                      ALU.subtract).then_inc(gT_lo, 1)
            si = sum_at(u, Y_LAG - 1)
            if si is not None and si % SUMS and within(n, SUMS, si):
                s = si % SUMS
                i = s - (0 if si > 0 else E_R)
                cnt(gate_done, E_R, i)
                part_free(cnt, si)
                dve.tensor_copy(part[:, s % 3, :], p_g[:, s % 2, :]).then_inc(gate_out, 1)
            si = sum_at(u, Y_LAG)
            if si is not None and within(n, SUMS, si):
                s = si % SUMS
                cnt(w2_done, U, end_of(s) + 1 - (U if si < 0 else 0))
                out, y = part[:, s % 3, :], p_y[:, s % RING_Y, :]
                if s == 0:
                    part_free(cnt, si)
                    ins = dve.tensor_scalar(out, y, t["b2T"][:, 0:1], t["b2T"][:, 1:2], ALU.add, ALU.add)
                else:
                    cnt(gate_out, E_R, s - (0 if si > 0 else E_R))
                    ins = dve.scalar_tensor_tensor(out=out, in0=y, scalar=t["b2T"][:, E_S + s - 1:E_S + s],
                                                   in1=out, op0=ALU.add, op1=ALU.mult)
                ins.then_inc(y_gated, 1)
            if u == BACK + 1 and within(n, 1, -1):
                cnt(back_done, 1, 0)
                cnt(stored, 16, -16)
                dve.tensor_tensor(res[:], p_t[:, 0, :].rearrange("p (q c) -> p q c", c=C),
                                  t["modB"][:, 3, ds(n - 1, 1), :].to_broadcast([P, QB, C]), ALU.mult
                                  ).then_inc(res_ready, 1)
                cnt(res_ready, 2, -1)
                dve.tensor_tensor(res[:], res[:], t["x"][:, ds((n - 1) * QB, QB), :], ALU.add).then_inc(res_ready, 1)

        def pool_block(pool, n):
            cnt = Count(pool, n)
            for s in range(1, SUMS):
                if s == 4:
                    cnt(gT_done, 1, 1)
                    pool.tensor_copy(gq[:], t["gate"][:, ds((n + 1) * QB, QB), :]).then_inc(gq_ready, 1)
                cnt(y_gated, SUMS, s + 1)
                if s == 1:
                    cnt(back_done, 1, 0)
                else:
                    cnt(acc_done, E_R, s - 1)
                first = part[:, 0, :] if s == 1 else acc
                pool.tensor_tensor(acc, first, part[:, s % 3, :], ALU.add).then_inc(acc_done, 1)

        block = ctx.enter_context(nc.Block())

        @block.gpsimd
        def _(pool):
            for e in range(E):
                pool.wait_ge(t["w_loaded"][e % RING_W], 32 * (e // RING_W + 1))
                k = 0 if e < E_S else 1
                pool.tensor_scalar(raw_of(e)[0], raw_of(e)[0], t["g2"][:, k:k + 1], 1.0, ALU.mult,
                                   ALU.mult).then_inc(w_scaled, 1)
                if e == 0:
                    pool.tensor_copy(gq[:], t["gate"][:, 0:QB, :]).then_inc(gq_ready, 1)
            pool_block(pool, 0)
            with pool.Fori(1, BATCH) as n:
                pool_block(pool, n)

        @block.tensor
        def _(pe):
            for u in range(U):
                pe_unit(pe, 0, u)
            with pe.Fori(1, BATCH) as n:
                for u in range(U):
                    pe_unit(pe, n, u)
            for u in range(BACK + 1):
                pe_unit(pe, BATCH, u)

        @block.scalar
        def _(act):
            act.preload_act_table_set("gelu_and_others")
            act_weights(act, 0, 0)
            act_weights(act, 0, 1)
            for u in range(U):
                act_unit(act, 0, u)
                if u % HT in W_AT and u // HT + 1 < E:
                    act_weights(act, u // HT + 1, W_AT.index(u % HT))
            with act.Fori(1, BATCH) as n:
                for u in range(U):
                    act_unit(act, n, u)
            act_unit(act, BATCH, 0)

        @block.vector
        def _(dve):
            dve_weights(dve, 0, 0)
            dve_weights(dve, 0, 1)
            dve.tensor_scalar(gT[:].rearrange("p (q c) -> p q c", q=QB), t["ident"][:].unsqueeze(1).to_broadcast([P, QB, P]),
                              0.0, None, ALU.mult).then_inc(sel_ready, 1)
            dve.tensor_tensor(sel[:], t["ident"][:, 0:E_R].unsqueeze(2).to_broadcast([P, E_R, P]),
                              t["ident"][:, LOW:LOW + E_R].unsqueeze(2).to_broadcast([P, E_R, P]),
                              ALU.add).then_inc(sel_ready, 1)
            for u in range(U):
                dve_unit(dve, 0, u)
                if u % HT in W_AT and u // HT + 1 < E:
                    dve_weights(dve, u // HT + 1, W_AT.index(u % HT))
            with dve.Fori(1, BATCH) as n:
                for u in range(U):
                    dve_unit(dve, n, u)
            for u in range(BACK + 2):
                dve_unit(dve, BATCH, u)

        @block.sync
        def _(sp):
            for e in range(RING_W, E):
                sp.wait_ge(w_lo, 2 * (e - RING_W + 1))
                load_expert(sp, t, dram, e)
            out = dram["out"].rearrange("(b q p) c -> b p q c", q=QB, p=P)
            with sp.Fori(0, BATCH) as b:
                sp.wait_ge(res_ready, b * 2 + 2)
                sp.dma_start(out[ds(b, 1)].rearrange("b p q c -> (b p) q c"), res[:]).then_inc(stored, 16)
            sp.wait_ge(stored, 16 * BATCH)


def program(nc, dram):
    with ExitStack() as ctx:
        t = {}

        def keep(name, shape, dt=F32):
            t[name] = ctx.enter_context(nc.sbuf_tensor("t_" + name, shape, dt))

        keep("ident", [P, P])
        keep("x", [P, QUADS, C])
        keep("hT", [P, QUADS + 2, P])
        keep("modB", [P, 4, BATCH, C])
        for name in ("mean", "var", "rstd"):
            keep(name, [P, QUADS])
        keep("stats", [P, QUADS, 6])
        keep("saT", [P, BATCH])
        keep("caT", [P, BATCH])
        for name in ("unH", "unL"):
            keep(name, [P, QUADS * P], F32R)
        keep("b1", [P, E * HT])
        keep("b2T", [P, E])
        keep("cent", [P, E_R])
        keep("g2", [P, 2])
        keep("lower", [P, E_R, E_R])
        keep("gate", [P, QUADS + QB, E_R])
        t["w_loaded"] = [ctx.enter_context(nc.semaphore("w_loaded%d" % i)) for i in range(RING_W)]
        with ExitStack() as first:
            for name in ("wq", "wk", "wv", "wo"):
                t[name] = first.enter_context(nc.sbuf_tensor("t_" + name, [P, CHUNKS * DH], F32))
            prepare(nc, t, dram)
            attend(nc, t, dram)
        for name in ("w1H", "w1L", "w2H", "w2L"):
            keep(name, [P, E, HID], F32R)
        mix(nc, t, dram)


def kernel(L0_attn_x, L0_attn_wq, L0_attn_wk, L0_attn_wv, L0_attn_wo, L0_ffn_g_shared, L0_ffn_W1_s, L0_ffn_b1_s,
           L0_ffn_W2_s, L0_ffn_b2_s, L0_ffn_g_routed, L0_ffn_W1_r, L0_ffn_b1_r, L0_ffn_W2_r, L0_ffn_b2_r,
           L0_ffn_centroids, L0_c, L0_wmod):
    import numpy as np
    import concourse.bacc as bacc
    from concourse.bass_utils import run_bass_kernel_spmd

    a = lambda v: np.asarray(v)
    arrays = {
        "x": a(L0_attn_x).reshape(BATCH * SEQ, C),
        "wqT": a(L0_attn_wq).T, "wkT": a(L0_attn_wk).T, "wvT": a(L0_attn_wv).T,
        "woT": a(L0_attn_wo).T.reshape(CHUNKS // 2, P, C).transpose(1, 0, 2).reshape(P, CHUNKS // 2 * C),
        "cT": a(L0_c).T, "wmod": a(L0_wmod),
        "g2": np.stack([a(L0_ffn_g_shared), a(L0_ffn_g_routed)], axis=1),
        "w1s": a(L0_ffn_W1_s), "w2s": a(L0_ffn_W2_s), "w1r": a(L0_ffn_W1_r), "w2r": a(L0_ffn_W2_r),
        "b1": np.concatenate([a(L0_ffn_b1_s), a(L0_ffn_b1_r)]).reshape(E * HT, P).T,
        "b2T": np.concatenate([a(L0_ffn_b2_s), a(L0_ffn_b2_r)]).T, "cent": a(L0_ffn_centroids),
    }
    arrays = {k + "_dram": np.ascontiguousarray(v) for k, v in arrays.items()}
    nc = bacc.Bacc("TRN2", target_bir_lowering=False, num_devices=1)
    dram = {k[:-5]: nc.dram_tensor(k, v.shape, F32, kind="ExternalInput").ap() for k, v in arrays.items()}
    dram["out"] = nc.dram_tensor("out_dram", (BATCH * SEQ, C), F32, kind="ExternalOutput").ap()
    program(nc, dram)
    r = run_bass_kernel_spmd(nc, [arrays], core_ids=[0])
    return r.results[0]["out_dram"].reshape(BATCH, SEQ, C)
```
